# Optimizing a Trainium2 kernel written in Bass

```python
import numpy as np
import jax
import jax.numpy as jnp

def _softmax(x, axis=-1):
    return jax.nn.softmax(x, axis=axis)

def _gelu(x):
    return jax.nn.gelu(x, approximate=True)

def _silu(x):
    return jax.nn.silu(x)

def _sigmoid(x):
    return jax.nn.sigmoid(x)

def _layernorm(x, axis=-1, eps=1e-05):
    m = jnp.mean(x, axis=axis, keepdims=True)
    v = jnp.var(x, axis=axis, keepdims=True)
    return (x - m) / jnp.sqrt(v + eps)

def _scatter_add(tgt, idx, src, axis=0):
    return tgt.at[idx].add(src)

def _segment_sum(src, seg, n):
    return jax.ops.segment_sum(src, seg, n)
kernel_name = 'mk_xattn_ffn_d1_seqx_r4_273970'

def setup_inputs(seed: int=0):
    np.random.seed(seed)
    _w = jnp.asarray

    def _rec_inputs():
        import jax
        import jax.numpy as jnp
        _rk = jax.random.key(seed)
        x = 7.22e-05 + 1 * jax.random.normal(jax.random.fold_in(_rk, 1), (2, 1024, 256), jnp.float32)
        _lenS = 1024 - jax.random.randint(jax.random.fold_in(_rk, 7), (2,), 0, max(1, 1024 // 4) + 1, jnp.int32)
        _lenS2 = 154 - jax.random.randint(jax.random.fold_in(_rk, 8), (2,), 0, max(1, 154 // 4) + 1, jnp.int32)
        _ctx_768P = jax.random.normal(jax.random.fold_in(_rk, 11), (2, 16, 192), jnp.float32)
        _ctx_768c = jax.random.dirichlet(jax.random.fold_in(_rk, 511), 0.3 * jnp.ones((16,), jnp.float32), (2, 154))
        _ctx_768t = jnp.einsum('bsk,bkd->bsd', _ctx_768c, _ctx_768P)
        _ctx_768t = _ctx_768t * jax.lax.rsqrt(jnp.mean(jnp.square(_ctx_768t)) + 1e-12) * 0.953939
        ctx_768 = 2.09791e-05 + 1.00001 * (_ctx_768t + 0.3 * jax.random.normal(jax.random.fold_in(_rk, 611), (2, 154, 192), jnp.float32))
        return (x, ctx_768)
    x, ctx_768 = _rec_inputs()

    def _L0_xattn_setup():
        import jax, jax.numpy as jnp
        import numpy as np
        NUM_HEADS = 16
        key = jax.random.key(seed)
        ks = jax.random.split(key, 8)
        dim, cond_dim = (256, 192)
        B, N, condN = (4, 512, 256)
        s = lambda k, shp, fan: jax.random.normal(k, shp, dtype=jnp.float32) * fan ** (-0.5)
        return {'x': jax.random.normal(ks[0], (B, N, dim), dtype=jnp.float32), 'cond': jax.random.normal(ks[1], (B, condN, cond_dim), dtype=jnp.float32), 'q_w': s(ks[2], (dim, dim), dim), 'q_b': jnp.zeros((dim,), jnp.float32), 'kv_w': s(ks[3], (cond_dim, 2 * dim), cond_dim), 'kv_b': jnp.zeros((2 * dim,), jnp.float32), 'proj_w': s(ks[4], (dim, dim), dim), 'proj_b': jnp.zeros((dim,), jnp.float32)}
    _L0_xattn_all = _L0_xattn_setup()
    _L0_xattn_in = {k: v for k, v in _L0_xattn_all.items() if k in ('q_w', 'q_b', 'kv_w', 'kv_b', 'proj_w', 'proj_b')}
    del _L0_xattn_all

    def _L0_ffn_setup():
        import jax, jax.numpy as jnp
        import numpy as np
        DIM = 256

        def _reference_tuple_inner(x, W_r, W_k, W_v, mu_r, mu_k):
            B, T, C = x.shape
            x_prev = jnp.concatenate([jnp.zeros((B, 1, C), x.dtype), x[:, :-1, :]], axis=1)
            xr = mu_r * x + (1.0 - mu_r) * x_prev
            xk = mu_k * x + (1.0 - mu_k) * x_prev
            r = jax.nn.sigmoid(jnp.einsum('btc,dc->btd', xr, W_r))
            k = jnp.einsum('btc,dc->btd', xk, W_k)
            k_act = jnp.square(jax.nn.relu(k))
            out = r * jnp.einsum('btc,dc->btd', k_act, W_v)
            new_state = x[:, -1, :]
            return (out, new_state)
        key = jax.random.key(seed)
        ks = jax.random.split(key, 6)
        B, T, C = (8, 512, DIM)
        x = jax.random.normal(ks[0], (B, T, C), dtype=jnp.float32)
        s = 1.0 / np.sqrt(C)
        W_r = jax.random.uniform(ks[1], (C, C), jnp.float32, -s, s)
        W_k = jax.random.uniform(ks[2], (C, C), jnp.float32, -s, s)
        W_v = jax.random.uniform(ks[3], (C, C), jnp.float32, -s, s)
        mu_r = jax.random.uniform(ks[4], (C,), jnp.float32)
        mu_k = jax.random.uniform(ks[5], (C,), jnp.float32)
        return {'x': x, 'W_r': W_r, 'W_k': W_k, 'W_v': W_v, 'mu_r': mu_r, 'mu_k': mu_k}
    _L0_ffn_all = _L0_ffn_setup()
    _L0_ffn_in = {k: v for k, v in _L0_ffn_all.items() if k in ('W_r', 'W_k', 'W_v', 'mu_r', 'mu_k')}
    del _L0_ffn_all
    return {'x': x, 'ctx_768': ctx_768, 'L0_xattn_q_w': _L0_xattn_in['q_w'], 'L0_xattn_q_b': _L0_xattn_in['q_b'], 'L0_xattn_kv_w': _L0_xattn_in['kv_w'], 'L0_xattn_kv_b': _L0_xattn_in['kv_b'], 'L0_xattn_proj_w': _L0_xattn_in['proj_w'], 'L0_xattn_proj_b': _L0_xattn_in['proj_b'], 'L0_ffn_W_r': _L0_ffn_in['W_r'], 'L0_ffn_W_k': _L0_ffn_in['W_k'], 'L0_ffn_W_v': _L0_ffn_in['W_v'], 'L0_ffn_mu_r': _L0_ffn_in['mu_r'], 'L0_ffn_mu_k': _L0_ffn_in['mu_k']}

def reference(x, ctx_768, L0_xattn_q_w, L0_xattn_q_b, L0_xattn_kv_w, L0_xattn_kv_b, L0_xattn_proj_w, L0_xattn_proj_b, L0_ffn_W_r, L0_ffn_W_k, L0_ffn_W_v, L0_ffn_mu_r, L0_ffn_mu_k):
    import jax
    import jax.numpy as jnp

    def _L0_xattn_ref(x, cond, q_w, q_b, kv_w, kv_b, proj_w, proj_b):
        import jax, jax.numpy as jnp
        import numpy as np
        NUM_HEADS = 16
        B, N, C = x.shape
        condN = cond.shape[1]
        H = NUM_HEADS
        hd = C // H
        scale = hd ** (-0.5)
        q = (x @ q_w + q_b).reshape(B, N, H, hd).transpose(0, 2, 1, 3)
        kv = (cond @ kv_w + kv_b).reshape(B, condN, 2, H, hd)
        k = kv[:, :, 0].transpose(0, 2, 1, 3)
        v = kv[:, :, 1].transpose(0, 2, 1, 3)
        attn = jnp.einsum('bhnd,bhmd->bhnm', q * scale, k)
        attn = jax.nn.softmax(attn, axis=-1)
        out = jnp.einsum('bhnm,bhmd->bhnd', attn, v)
        out = out.transpose(0, 2, 1, 3).reshape(B, N, C)
        return out @ proj_w + proj_b

    def _L0_ffn_ref(x, W_r, W_k, W_v, mu_r, mu_k):
        import jax, jax.numpy as jnp
        import numpy as np
        DIM = 256

        def _reference_tuple_inner(x, W_r, W_k, W_v, mu_r, mu_k):
            B, T, C = x.shape
            x_prev = jnp.concatenate([jnp.zeros((B, 1, C), x.dtype), x[:, :-1, :]], axis=1)
            xr = mu_r * x + (1.0 - mu_r) * x_prev
            xk = mu_k * x + (1.0 - mu_k) * x_prev
            r = jax.nn.sigmoid(jnp.einsum('btc,dc->btd', xr, W_r))
            k = jnp.einsum('btc,dc->btd', xk, W_k)
            k_act = jnp.square(jax.nn.relu(k))
            out = r * jnp.einsum('btc,dc->btd', k_act, W_v)
            new_state = x[:, -1, :]
            return (out, new_state)
        return _reference_tuple_inner(x, W_r, W_k, W_v, mu_r, mu_k)[0]
    x = x + _L0_xattn_ref(_layernorm(x, axis=-1), ctx_768, L0_xattn_q_w, L0_xattn_q_b, L0_xattn_kv_w, L0_xattn_kv_b, L0_xattn_proj_w, L0_xattn_proj_b)
    x = x + _L0_ffn_ref(_layernorm(x, axis=-1), L0_ffn_W_r, L0_ffn_W_k, L0_ffn_W_v, L0_ffn_mu_r, L0_ffn_mu_k)
    return x

_drawn_inputs = setup_inputs


def setup_inputs(seed=0):
    import zlib

    import numpy as np

    out = dict(_drawn_inputs(seed))
    spreads = {'L0_xattn_q_b': (0.0, 0.356), 'L0_xattn_kv_b': (0.0, 0.1), 'L0_xattn_proj_b': (0.0, 0.1)}
    factors = {'L0_ffn_W_r': 3.215, 'L0_ffn_mu_r': 7.55}
    for name, (base, spread) in spreads.items():
        noise = np.random.default_rng([zlib.crc32(name.encode()), seed]).standard_normal(out[name].shape)
        drawn = base * np.exp(spread * noise) if base else spread * noise
        out[name] = jnp.asarray(drawn.astype(out[name].dtype))
    for name, factor in factors.items():
        out[name] = (out[name] * factor).astype(out[name].dtype)
    return out
```

```python
from contextlib import ExitStack

import concourse.bass as bass
import concourse.mybir as mybir

F32 = mybir.dt.float32
BF16 = mybir.dt.bfloat16
ALU = mybir.AluOpType
ACT = mybir.ActivationFunctionType
AX_X = mybir.AxisListType.X

P = 128
BATCH, SEQ, DIM = 2, 1024, 256
CTX, CDIM = 154, 192
HEADS, HD = 16, 16
TILE = 512
TILES = BATCH * SEQ // TILE
TB = SEQ // TILE
SUB = TILE // P
CC = DIM // P
REST = CTX - P
CPAD = P + 32
QPARTS = (0, 0, 1, 0, 2, 1)
KPARTS = (0, 1, 0, 2, 0, 1)
STACK = 16 * len(QPARTS)
DEPTH = STACK + 3
UNITS = HEADS // 4
GROUPS = ((0, 3), (3, 3), (6, 3), (9, 3), (12, 2), (14, 2))
NG = len(GROUPS)
KD = (P, CDIM - P)
EPS = 1e-5
QSCALE = HD ** -0.5


def schedule():
    s = [("ln1", 0), ("kv",), ("q", 0), ("ln1", 1)]
    s += [("max", 0, t) for t in range(SUB)]
    s += [("maxrows", 0), ("q", 1)]
    for i in range(TILES + 1):
        for u in range(UNITS):
            if i < TILES:
                s.append(("attn", i, u))
            elif u == 0:
                s.append(("flush",))
            if u == 0 and i >= 1:
                s.append(("recip", i - 1))
            if u == 0 and i >= 2:
                s.append(("mix", i - 2))
            if u == 0 and i + 2 < TILES:
                s.append(("ln1", i + 2))
            if u == 1 and i >= 1:
                s.append(("scale", i - 1))
            if u == 1 and i + 2 < TILES:
                s.append(("q", i + 2))
            if u == 1 and i == TILES:
                s.append(("out", i - 2))
            if u == 2 and i >= 1:
                s.append(("proj", i - 1))
            if u == 3 and i + 1 < TILES:
                s.append(("maxrows", i + 1))
            if u == 3 and i >= 1:
                s.append(("ln2t", i - 1))
            if u == 3 and 2 <= i < TILES:
                s.append(("out", i - 2))
    s += [("mix", TILES - 1), ("out", TILES - 1)]
    return s


def shared_bank_uses(steps):
    uses = {"kv": [("k", 0), ("k", 1), ("vmain",), ("vrest",)], "q": [("xt", 0), ("xt", 1), ("q", 0), ("q", 1)],
            "maxrows": [("maxt",)], "proj": [("proj", 0), ("proj", 1)], "ln2t": [("x2t", 0), ("x2t", 1)],
            "mix": [("key", 0), ("key", 1), ("gate", 0), ("gate", 1)], "out": [("val", 0), ("val", 1)]}
    number = {}
    for s in steps:
        for use in uses.get(s[0], ()):
            number[use + tuple(s[1:])] = len(number)
    return number


def build(nc, x, ctx_t, q_w, vecs, kv_w, kv_b, proj_w, proj_b, wr_t, wk_t, wv_t, out):
    STEPS = schedule()
    USE = shared_bank_uses(STEPS)

    with ExitStack() as stack:
        def sb(name, shape, dt=F32):
            return stack.enter_context(nc.sbuf_tensor(name, shape, dt))

        def ps(name, shape, dt=F32):
            return stack.enter_context(nc.psum_tensor(name, shape, dt))

        def sem(name):
            return stack.enter_context(nc.semaphore(name))

        x_nat = sb("x_nat", [P, TILES, SUB, DIM])
        xn = sb("xn", [P, SUB, DIM])
        xnT = sb("xnT", [P, CC, TILE])
        wq = sb("wq", [P, CC, DIM])
        wkv = sb("wkv", [P, 2, 2 * DIM])
        wp = sb("wp", [P, CC, DIM])
        wr = sb("wr", [P, CC, DIM])
        wk = sb("wk", [P, CC, DIM])
        wv = sb("wv", [P, CC, DIM])
        ctxT = sb("ctxT", [P, 2, BATCH * CTX])
        cols = sb("cols", [P, 5, CC])
        vbias = sb("vbias", [P, DIM])
        pbias = sb("pbias", [P, DIM])
        ident = sb("ident", [P, P])
        identb = sb("identb", [P, P], BF16)
        stats = sb("stats", [P, SUB, 6])
        mv = sb("mv", [P, 2, SUB, 2])
        vare = sb("vare", [P, 2, SUB])
        rstd = sb("rstd", [P, 2, SUB])
        halves = sb("halves", [P, SUB])
        kf = sb("kf", [P, CC, BATCH * CTX])
        kr = sb("kr", [P, CC, BATCH * CTX])
        kparts = sb("kparts", [P, 3, CC, BATCH, CPAD], BF16)
        qf = sb("qf", [P, CC, TILE])
        qr = sb("qr", [P, CC, TILE])
        qparts = sb("qparts", [P, 3, CC, TILE], BF16)
        kstack = sb("kstack", [DEPTH, HEADS, BATCH, CPAD], BF16)
        qstack = sb("qstack", [DEPTH, 2, HEADS, TILE], BF16)
        vmain = sb("vmain", [P, BATCH, HEADS, 32])
        vrest = sb("vrest", [P, BATCH, UNITS, P])
        nmax = sb("nmax", [P, SUB, HEADS])
        nmaxr = sb("nmaxr", [P, SUB, HEADS])
        mparts = sb("mparts", [P, SUB, 3, HEADS], BF16)
        mT = sb("mT", [3 * HEADS, TILE], BF16)
        probs = sb("probs", [P, 2, 5, TILE])
        pvout = sb("pvout", [P, 2, TILE])
        sums = sb("sums", [P, 64])
        rsums = sb("rsums", [P, 64])
        attn = sb("attn", [P, CC, TILE])
        rbc = sb("rbc", [P, CC, TILE])
        x2 = sb("x2", [P, 2, SUB, DIM])
        xn2T = sb("xn2T", [P, 2, CC, TILE + 1])
        diff = sb("diff", [P, CC, TILE])
        xr = sb("xr", [P, CC, TILE])
        xk = sb("xk", [P, CC, TILE])
        kact = sb("kact", [P, CC, TILE])
        gate = sb("gate", [P, SUB, DIM])
        y = sb("y", [P, SUB, DIM])
        xn2 = y
        relu = diff

        kd = nc.dram_tensor("k_parts_d", [3, DIM, BATCH * CPAD], BF16, kind="Internal").ap()
        qd = nc.dram_tensor("q_parts_d", [2, 3, DIM, TILE], BF16, kind="Internal").ap()
        pvd = nc.dram_tensor("pv_d", [2, HEADS, 32, TILE], F32, kind="Internal").ap()
        rsd = nc.dram_tensor("rsums_d", [2, HEADS, TILE], F32, kind="Internal").ap()

        shared = [ps(f"shared{n}", [P, 512]) for n in range(2)]
        smax = [ps(f"smax{n}", [P, 512]) for n in range(2)]
        sexp = [ps(f"sexp{n}", [P, 512]) for n in range(3)]
        pv = ps("pv", [P, 512])

        x_in = [sem(f"x_in{t}") for t in range(TILES)]
        w_in = sem("w_in")
        wkv_in = sem("wkv_in")
        wlate_in = sem("wlate_in")
        const_ok = sem("const_ok")
        ones_ok = sem("ones_ok")
        filled = [sem(f"filled{n}") for n in range(2)]
        emptied = [sem(f"emptied{n}") for n in range(2)]
        v_step = sem("v_step")
        g_step = sem("g_step")
        a_step = sem("a_step")
        var_ok = sem("var_ok")
        rstd_ok = sem("rstd_ok")
        xn_ok = sem("xn_ok")
        xnT_ok = sem("xnT_ok")
        qf_ok = sem("qf_ok")
        kf_ok = sem("kf_ok")
        kparts_ok = sem("kparts_ok")
        kd_ok = sem("kd_ok")
        kstack_ok = sem("kstack_ok")
        v_ok = sem("v_ok")
        qparts_ok = sem("qparts_ok")
        qd_ok = [sem(f"qd_ok{n}") for n in range(2)]
        qstack_ok = [sem(f"qstack_ok{n}") for n in range(2)]
        smax_full = sem("smax_full")
        smax_read = sem("smax_read")
        mparts_ok = sem("mparts_ok")
        mT_ok = sem("mT_ok")
        mrows_ok = [sem(f"mrows_ok{n}") for n in range(2)]
        sexp_full = sem("sexp_full")
        exp_ok = sem("exp_ok")
        pv_full = sem("pv_full")
        pvout_ok = sem("pvout_ok")
        pvd_ok = [sem(f"pvd_ok{n}") for n in range(2)]
        sums_ok = [sem(f"sums_ok{n}") for n in range(2)]
        rsums_ok = sem("rsums_ok")
        rsd_ok = [sem(f"rsd_ok{n}") for n in range(2)]
        rbc_ok = [sem(f"rbc_ok{n}") for n in range(2)]
        attn_in = [sem(f"attn_in{n}") for n in range(2)]
        attn_ok = sem("attn_ok")
        x2_ok = sem("x2_ok")
        resid_ok = sem("resid_ok")
        xn2_ok = sem("xn2_ok")
        xn2T_ok = sem("xn2T_ok")
        diff_ok = sem("diff_ok")
        mixed_ok = sem("mixed_ok")
        kact_ok = sem("kact_ok")
        gate_ok = sem("gate_ok")
        y_ok = sem("y_ok")
        y_out = sem("y_out")

        x_d = x.rearrange("b (t s p) c -> (b t) p s c", s=SUB, p=P)
        out_d = out.rearrange("b (t s p) c -> (b t) p s c", s=SUB, p=P)

        def bank(*use):
            return shared[USE[use] % 2]

        def may_fill(eng, *use):
            n = USE[use]
            if n >= 2:
                eng.wait_ge(emptied[n % 2], n // 2)

        def fill(ins, *use):
            ins.then_inc(filled[USE[use] % 2], 1)

        def await_bank(eng, *use):
            n = USE[use]
            eng.wait_ge(filled[n % 2], n // 2 + 1)

        def empty(ins, *use):
            ins.then_inc(emptied[USE[use] % 2], 1)

        block = stack.enter_context(nc.Block())

        @block.sync
        def _(sp):
            sp.dma_start(x_nat[:, 0], x_d[0]).then_inc(x_in[0], 16)
            for k in range(2):
                sp.dma_start(ctxT[0:KD[k], k, :], ctx_t[k * P:k * P + KD[k], :]).then_inc(wkv_in, 16)
                sp.dma_start(wkv[0:KD[k], k, :], kv_w[k * P:k * P + KD[k], :]).then_inc(wkv_in, 16)
            sp.dma_start(cols[:, 0:4, :], vecs).then_inc(w_in, 16)
            sp.dma_start(wq[:, :, :], q_w.rearrange("(c p) n -> p c n", p=P)).then_inc(w_in, 16)
            sp.dma_start(vbias[:, :], kv_b[DIM:2 * DIM].partition_broadcast(P)).then_inc(w_in, 16)
            sp.dma_start(x_nat[:, 1], x_d[1]).then_inc(x_in[1], 16)

            for s in STEPS:
                stage, T = s[0], (s[1] if len(s) > 1 else 0)
                if stage == "kv":
                    sp.wait_ge(kparts_ok, 1)
                    sp.dma_start(kd.rearrange("a (m p) n -> p a m n", p=P),
                                 kparts[:, :, :, :, :].rearrange("p a m b n -> p a m (b n)")).then_inc(kd_ok, 16)
                    sp.wait_ge(kd_ok, 16)
                    for g, part in enumerate(KPARTS):
                        sp.dma_start(kstack[16 * g:16 * g + 16, :, :, :].rearrange("p h b n -> p h (b n)"),
                                     kd[part].rearrange("(h d) n -> d h n", d=HD)).then_inc(kstack_ok, 16)
                if stage == "q":
                    sp.wait_ge(qparts_ok, T + 1)
                    sp.dma_start(qd[T % 2].rearrange("a (m p) n -> p a m n", p=P), qparts[:, :, :, :]).then_inc(qd_ok[T % 2], 16)
                    sp.wait_ge(qd_ok[T % 2], 16 * (T // 2 + 1))
                    if T >= 2:
                        sp.wait_ge(sexp_full, 5 * UNITS * (T - 1))
                    for g, part in enumerate(QPARTS):
                        sp.dma_start(qstack[16 * g:16 * g + 16, T % 2],
                                     qd[T % 2, part].rearrange("(h d) n -> d h n", d=HD)).then_inc(qstack_ok[T % 2], 16)
                    if T == 0:
                        for w_sb, w_d in ((wp, proj_w), (wr, wr_t), (wk, wk_t), (wv, wv_t)):
                            sp.dma_start(w_sb[:, :, :], w_d.rearrange("(c p) n -> p c n", p=P)).then_inc(wlate_in, 16)
                        sp.dma_start(pbias[:, :], proj_b.partition_broadcast(P)).then_inc(wlate_in, 16)
                        for t in range(2, TILES):
                            sp.dma_start(x_nat[:, t], x_d[t]).then_inc(x_in[t], 16)
                if stage == "maxrows":
                    sp.wait_ge(mT_ok, T + 1)
                    for part in range(3):
                        sp.dma_start(qstack[STACK + part:STACK + part + 1, T % 2, :, :],
                                     mT[part * HEADS:(part + 1) * HEADS, :]).then_inc(mrows_ok[T % 2], 16)
                if stage in ("attn", "flush"):
                    U = (s[1] * UNITS + s[2] if stage == "attn" else TILES * UNITS) - 1
                    if U >= 0:
                        t, u = U // UNITS, U % UNITS
                        sp.wait_ge(pvout_ok, U + 1)
                        sp.dma_start(pvd[t % 2, 4 * u:4 * u + 4].rearrange("h r n -> (h r) n"),
                                     pvout[:, U % 2, :]).then_inc(pvd_ok[U % 2], 16)
                if stage == "recip":
                    for n in range(2):
                        sp.wait_ge(pvd_ok[n], 16 * UNITS // 2 * (T + 1))
                    if T >= 1:
                        sp.wait_ge(rsums_ok, T)
                    sp.dma_start(sums[:, :], pvd[T % 2, :, HD, :].rearrange("h (c n) -> h c n", n=64)).then_inc(sums_ok[T % 2], 16)
                    if T >= 1:
                        sp.wait_ge(x2_ok, SUB // 2 * T)
                    for c in range(CC):
                        sp.dma_start(attn[:, c, :], pvd[T % 2, 8 * c:8 * c + 8, 0:HD, :]).then_inc(attn_in[T % 2], 16)
                if stage == "scale":
                    sp.wait_ge(rsums_ok, T + 1)
                    sp.dma_start(rsd[T % 2].rearrange("h (c n) -> h c n", n=64), rsums[:, :]).then_inc(rsd_ok[T % 2], 16)
                    sp.wait_ge(rsd_ok[T % 2], 16 * (T // 2 + 1))
                    if T >= 1:
                        sp.wait_ge(attn_ok, T)
                    for c in range(CC):
                        sp.dma_start(rbc[:, c, :],
                                     rsd[T % 2, 8 * c:8 * c + 8, :].rearrange("h (o n) -> h o n", o=1).to_broadcast([8, HD, TILE])
                                     ).then_inc(rbc_ok[T % 2], 16)
                if stage == "out":
                    sp.wait_ge(y_ok, T + 1)
                    sp.dma_start(out_d[T], y[:, :, :]).then_inc(y_out, 16)
            sp.wait_ge(y_out, 16 * TILES)

        @block.gpsimd
        def _(pool):
            steps = [0]

            def step(ins):
                ins.then_inc(g_step, 1)
                steps[0] += 1
                pool.wait_ge(g_step, steps[0])

            nc.gpsimd.memset(halves[:, :], -0.5)
            nc.gpsimd.memset(identb[:, :], 0.0)
            step(nc.gpsimd.memset(ident[:, :], 0.0))
            for m in (ident, identb):
                last = nc.gpsimd.affine_select(out=m[:, :], in_=m[:, :], compare_op=ALU.not_equal, fill=1.0,
                                               base=0, pattern=[[-1, P]], channel_multiplier=1)
            last.then_inc(const_ok, 1)
            step(nc.gpsimd.memset(kparts[:, :, :, :, CTX:CPAD], 0.0))
            step(nc.gpsimd.memset(kstack[STACK:DEPTH, :, :, CTX:CPAD], 0.0))
            step(nc.gpsimd.memset(kstack[STACK:DEPTH, :, :, 0:CTX], 1.0))
            nc.gpsimd.memset(vmain[:, :, :, HD:32], 1.0)
            step(nc.gpsimd.memset(vrest[:, :, :, :], 0.0))
            for j in range(4):
                step(nc.gpsimd.memset(vrest[32 * j:32 * j + REST, :, :, 32 * j + HD:32 * j + 32], 1.0))
            nc.gpsimd.memset(xn2T[:, 0, :, 0:1], 0.0).then_inc(ones_ok, 1)

            norms = [0]

            def rsqrt(which):
                norms[0] += 1
                pool.wait_ge(var_ok, norms[0])
                nc.gpsimd.tensor_tensor(rstd[:, which, :], vare[:, which, :], halves[:, :], ALU.pow).then_inc(rstd_ok, 1)

            for s in STEPS:
                stage, T = s[0], (s[1] if len(s) > 1 else 0)
                if stage == "ln1":
                    rsqrt(0)
                if stage == "proj":
                    rsqrt(1)
                if stage == "q":
                    pool.wait_ge(xn_ok, T + 1)
                    if T == 0:
                        pool.wait_ge(wlate_in, 16 * 5)
                    for t in range(SUB):
                        last = nc.gpsimd.tensor_tensor(x_nat[:, T, t, :], x_nat[:, T, t, :], pbias[:, :], ALU.add)
                    last.then_inc(resid_ok, 1)
                if stage == "ln2t":
                    if T % TB:
                        pool.wait_ge(xn2T_ok, CC * (T + 1))
                        step(nc.gpsimd.tensor_copy(xn2T[:, T % 2, :, 0:1], xn2T[:, (T - 1) % 2, :, TILE:TILE + 1]))
                    for c in range(CC):
                        pool.wait_ge(xn2T_ok, CC * T + c + 1)
                        if T >= 1:
                            pool.wait_ge(kact_ok, CC * T)
                        nc.gpsimd.tensor_tensor(diff[:, c, :], xn2T[:, T % 2, c, 1:TILE + 1], xn2T[:, T % 2, c, 0:TILE],
                                                ALU.subtract).then_inc(diff_ok, 1)

        @block.scalar
        def _(act):
            def unit_done(U):
                act.wait_ge(pv_full, U + 1)
                if U >= 2:
                    act.wait_ge(pvd_ok[U % 2], 16 * (U // 2))
                nc.scalar.copy(pvout[:, U % 2, :], pv[:, :]).then_inc(pvout_ok, 1)

            for s in STEPS:
                stage, T = s[0], (s[1] if len(s) > 1 else 0)
                if stage == "kv":
                    act.wait_ge(w_in, 16 * 3)
                    for m in range(CC):
                        await_bank(act, "k", m)
                        empty(nc.scalar.activation(kf[:, m, :], bank("k", m)[:, 0:BATCH * CTX], ACT.Identity,
                                                   bias=cols[:, 1, m:m + 1]), "k", m)
                if stage == "q":
                    for c in range(CC):
                        await_bank(act, "xt", c, T)
                        if T >= 1 and c == 0:
                            act.wait_ge(filled[USE[("q", 1, T - 1)] % 2], USE[("q", 1, T - 1)] // 2 + 1)
                        empty(nc.scalar.copy(xnT[:, c, :], bank("xt", c, T)[:, :]), "xt", c, T)
                    if T == 0:
                        act.wait_ge(a_step, 1)
                    for m in range(CC):
                        await_bank(act, "q", m, T)
                        if T >= 1:
                            act.wait_ge(qparts_ok, T)
                        empty(nc.scalar.activation(qf[:, m, :], bank("q", m, T)[:, :], ACT.Identity,
                                                   bias=cols[:, 4, m:m + 1], scale=QSCALE), "q", m, T)
                if stage == "attn":
                    i, u = s[1:]
                    U = i * UNITS + u
                    for c in range(5):
                        n = 5 * U + c
                        act.wait_ge(sexp_full, n + 1)
                        if U >= 2 and c == 0:
                            act.wait_ge(pv_full, U - 1)
                        nc.scalar.activation(probs[:, U % 2, c, :], sexp[n % 3][:, :], ACT.Exp).then_inc(exp_ok, 1)
                    if U >= 1:
                        unit_done(U - 1)
                if stage == "flush":
                    unit_done(TILES * UNITS - 1)
                if stage == "ln2t":
                    for c in range(CC):
                        await_bank(act, "x2t", c, T)
                        if T >= 2:
                            act.wait_ge(mixed_ok, CC * (T - 1))
                        ins = nc.scalar.copy(xn2T[:, T % 2, c, 1:TILE + 1], bank("x2t", c, T)[:, :])
                        ins.then_inc(xn2T_ok, 1)
                        act.wait_ge(xn2T_ok, CC * T + c + 1)
                        act.sem_inc(emptied[USE[("x2t", c, T)] % 2], 1)
                if stage == "mix":
                    for m in range(CC):
                        await_bank(act, "key", m, T)
                        act.wait_ge(mixed_ok, CC * (T + 1))
                        empty(nc.scalar.activation(relu[:, m, :], bank("key", m, T)[:, :], ACT.Relu), "key", m, T)
                        act.wait_ge(emptied[USE[("key", m, T)] % 2], USE[("key", m, T)] // 2 + 1)
                        if T >= 1:
                            act.wait_ge(y_ok, T)
                        nc.scalar.activation(kact[:, m, :], relu[:, m, :], ACT.Square).then_inc(kact_ok, 1)
                    for h in range(2):
                        await_bank(act, "gate", h, T)
                        empty(nc.scalar.activation(gate[:, 2 * h:2 * h + 2, :].rearrange("p s c -> p (s c)"),
                                                   bank("gate", h, T)[:, :], ACT.Tanh, scale=0.5), "gate", h, T)

        @block.vector
        def _(dve):
            steps = [0]

            def step(ins):
                ins.then_inc(v_step, 1)
                steps[0] += 1
                dve.wait_ge(v_step, steps[0])

            norms = [0]

            def layer_norm(which, source, target, done):
                for t in range(SUB):
                    last = nc.vector.bn_stats(out=stats[:, t, :], in_=source(t))
                step(last)
                for t in range(SUB):
                    last = nc.vector.bn_aggr(out=mv[:, which, t, :], in_=stats[:, t, :])
                step(last)
                nc.vector.tensor_scalar_add(vare[:, which, :], mv[:, which, :, 1], EPS).then_inc(var_ok, 1)
                norms[0] += 1
                dve.wait_ge(rstd_ok, norms[0])
                for t in range(SUB):
                    last = nc.vector.tensor_scalar(target[:, t, :], source(t), mv[:, which, t, 0:1],
                                                   rstd[:, which, t:t + 1], ALU.subtract, ALU.mult)
                last.then_inc(done, 1)

            def split(whole, left, parts):
                step(nc.vector.tensor_copy(parts[0], whole))
                step(nc.vector.tensor_tensor(left, whole, parts[0], ALU.subtract))
                step(nc.vector.tensor_copy(parts[1], left))
                return nc.vector.tensor_tensor(parts[2], left, parts[1], ALU.subtract)

            for s in STEPS:
                stage, T = s[0], (s[1] if len(s) > 1 else 0)
                if stage == "ln1":
                    dve.wait_ge(x_in[T], 16)
                    if T >= 1:
                        use = USE[("xt", 1, T - 1)]
                        dve.wait_ge(filled[use % 2], use // 2 + 1)
                    layer_norm(0, lambda t: x_nat[:, T, t, :], xn, xn_ok)
                if stage == "kv":
                    dve.wait_ge(w_in, 16 * 3)
                    nc.vector.tensor_scalar_mul(cols[:, 4, :], cols[:, 0, :], QSCALE).then_inc(a_step, 1)
                    for m in range(CC):
                        use = USE[("k", m)]
                        dve.wait_ge(emptied[use % 2], use // 2 + 1)
                    dve.wait_ge(ones_ok, 1)
                    kpart = [kparts[:, a, :, :, 0:CTX] for a in range(3)]
                    split(kf[:, :, :].rearrange("p m (b n) -> p m b n", b=BATCH),
                          kr[:, :, :].rearrange("p m (b n) -> p m b n", b=BATCH), kpart).then_inc(kparts_ok, 1)
                    await_bank(dve, "vmain")
                    for b in range(BATCH):
                        last = nc.vector.tensor_tensor(
                            vmain[:, b, :, 0:HD], bank("vmain")[:, b * DIM:(b + 1) * DIM].rearrange("p (h d) -> p h d", d=HD),
                            vbias[:, :].rearrange("p (h d) -> p h d", d=HD), ALU.add)
                    empty(last, "vmain")
                    await_bank(dve, "vrest")
                    for j in range(4):
                        rows = slice(32 * j, 32 * j + REST)
                        for b in range(BATCH):
                            last = nc.vector.tensor_tensor(
                                vrest[rows, b, :, 32 * j:32 * j + HD],
                                bank("vrest")[rows, b * 64:(b + 1) * 64].rearrange("p (g d) -> p g d", d=HD),
                                vbias[rows, :].rearrange("p (g j d) -> p j g d", j=4, d=HD)[:, j], ALU.add)
                    step(last)
                    dve.sem_inc(v_ok, 1)
                    dve.sem_inc(emptied[USE[("vrest",)] % 2], 1)
                if stage == "q":
                    for m in range(CC):
                        use = USE[("q", m, T)]
                        dve.wait_ge(emptied[use % 2], use // 2 + 1)
                    if T >= 1:
                        dve.wait_ge(qd_ok[(T - 1) % 2], 16 * ((T - 1) // 2 + 1))
                    split(qf[:, :, :], qr[:, :, :], [qparts[:, a] for a in range(3)]).then_inc(qparts_ok, 1)
                if stage == "max" or (stage == "attn" and T + 1 < TILES):
                    t = s[2]
                    T = T if stage == "max" else T + 1
                    for g, (h0, nh) in enumerate(GROUPS):
                        n = (T * SUB + t) * NG + g
                        dve.wait_ge(smax_full, n + 1)
                        if g == 0 and t == 0 and T >= 1:
                            dve.wait_ge(mparts_ok, T)
                        nc.vector.tensor_reduce(nmax[:, t, h0:h0 + nh],
                                                smax[n % 2][:, 0:nh * CTX].rearrange("p (h n) -> p h n", n=CTX),
                                                AX_X, ALU.max, negate=True).then_inc(smax_read, 1)
                if stage == "maxrows":
                    dve.wait_ge(smax_read, (T + 1) * SUB * NG)
                    if T >= 1:
                        use = USE[("maxt", T - 1)]
                        dve.wait_ge(filled[use % 2], use // 2 + 1)
                    split(nmax[:, :, :], nmaxr[:, :, :], [mparts[:, :, a, :] for a in range(3)]).then_inc(mparts_ok, 1)
                    await_bank(dve, "maxt", T)
                    if T >= 1:
                        dve.wait_ge(mrows_ok[(T - 1) % 2], 48 * ((T - 1) // 2 + 1))
                    ins = nc.vector.tensor_copy(mT[:, :], bank("maxt", T).bitcast(BF16)[0:3 * HEADS, 0:TILE])
                    step(ins)
                    dve.sem_inc(mT_ok, 1)
                    dve.sem_inc(emptied[USE[("maxt", T)] % 2], 1)
                if stage == "recip":
                    dve.wait_ge(sums_ok[T % 2], 16 * (T // 2 + 1))
                    if T >= 1:
                        dve.wait_ge(rsd_ok[(T - 1) % 2], 16 * ((T - 1) // 2 + 1))
                    nc.vector.reciprocal(rsums[:, :], sums[:, :]).then_inc(rsums_ok, 1)
                if stage == "scale":
                    dve.wait_ge(attn_in[T % 2], 32 * (T // 2 + 1))
                    dve.wait_ge(rbc_ok[T % 2], 32 * (T // 2 + 1))
                    nc.vector.tensor_tensor(attn[:, :, :], attn[:, :, :], rbc[:, :, :], ALU.mult).then_inc(attn_ok, 1)
                if stage == "proj":
                    dve.wait_ge(resid_ok, T + 1)
                    for h in range(2):
                        await_bank(dve, "proj", h, T)
                        ins = nc.vector.tensor_tensor(
                            x2[:, T % 2, 2 * h:2 * h + 2, :].rearrange("p s c -> p (s c)"), bank("proj", h, T)[:, :],
                            x_nat[:, T, 2 * h:2 * h + 2, :].rearrange("p s c -> p (s c)"), ALU.add)
                        ins.then_inc(x2_ok, 1)
                        dve.wait_ge(x2_ok, 2 * T + h + 1)
                        dve.sem_inc(emptied[USE[("proj", h, T)] % 2], 1)
                    stored = sum(r[0] == "out" for r in STEPS[:STEPS.index(s)])
                    if stored:
                        dve.wait_ge(y_out, 16 * stored)
                    layer_norm(1, lambda t: x2[:, T % 2, t, :], xn2, xn2_ok)
                if stage == "ln2t":
                    for c in range(CC):
                        dve.wait_ge(diff_ok, CC * T + c + 1)
                        if T >= 1 and c == 0:
                            use = USE[("gate", 1, T - 1)]
                            dve.wait_ge(filled[use % 2], use // 2 + 1)
                        for target, n in ((xr, 2), (xk, 3)):
                            last = nc.vector.scalar_tensor_tensor(
                                out=target[:, c, :], in0=diff[:, c, :], scalar=cols[:, n, c:c + 1],
                                in1=xn2T[:, T % 2, c, 0:TILE], op0=ALU.mult, op1=ALU.add)
                        last.then_inc(mixed_ok, 1)
                if stage == "out":
                    use = USE[("gate", 1, T)]
                    dve.wait_ge(emptied[use % 2], use // 2 + 1)
                    for h in range(2):
                        await_bank(dve, "val", h, T)
                        g2 = gate[:, 2 * h:2 * h + 2, :].rearrange("p s c -> p (s c)")
                        ins = nc.vector.scalar_tensor_tensor(out=g2, in0=g2, scalar=1.0, in1=bank("val", h, T)[:, :],
                                                             op0=ALU.add, op1=ALU.mult)
                        step(ins)
                        dve.sem_inc(emptied[USE[("val", h, T)] % 2], 1)
                    if T >= 1:
                        dve.wait_ge(y_out, 16 * T)
                    normed = sum(r[0] == "ln2t" for r in STEPS[:STEPS.index(s)])
                    use = USE[("x2t", 1, normed - 1)]
                    dve.wait_ge(filled[use % 2], use // 2 + 1)
                    nc.vector.scalar_tensor_tensor(out=y[:, :, :], in0=gate[:, :, :], scalar=0.5, in1=x2[:, T % 2, :, :],
                                                   op0=ALU.mult, op1=ALU.add).then_inc(y_ok, 1)

        @block.tensor
        def _(pe):
            def transposes(source, name, T):
                for c in range(CC):
                    may_fill(pe, name, c, T)
                    for t in range(SUB):
                        last = nc.tensor.transpose(bank(name, c, T)[:, t * P:(t + 1) * P],
                                                   source[:, t, c * P:(c + 1) * P], ident[:, :])
                    fill(last, name, c, T)

            def natural(name, lhs, w, T):
                for h in range(2):
                    may_fill(pe, name, h, T)
                    for t in range(2 * h, 2 * h + 2):
                        for k in range(CC):
                            last = nc.tensor.matmul(bank(name, h, T)[:, (t % 2) * DIM:(t % 2 + 1) * DIM],
                                                    lhs[:, k, t * P:(t + 1) * P], w[:, k, :],
                                                    start=(k == 0), stop=(k == CC - 1))
                    fill(last, name, h, T)

            def channels(name, w, rhs, T):
                for m in range(CC):
                    may_fill(pe, name, m, T)
                    for k in range(CC):
                        last = nc.tensor.matmul(bank(name, m, T)[:, :], w[:, k, m * P:(m + 1) * P], rhs[:, k, :],
                                                start=(k == 0), stop=(k == CC - 1))
                    fill(last, name, m, T)

            def max_scores(T, t, groups):
                for g in groups:
                    h0, nh = GROUPS[g]
                    n = (T * SUB + t) * NG + g
                    if n >= 2:
                        pe.wait_ge(smax_read, n - 1)
                    for k in range(nh):
                        last = nc.tensor.matmul(smax[n % 2][:, k * CTX:(k + 1) * CTX],
                                                qstack[0:STACK, T % 2, h0 + k, t * P:(t + 1) * P],
                                                kstack[0:STACK, h0 + k, T // TB, 0:CTX], start=True, stop=True)
                    last.then_inc(smax_full, 1)

            def values(U, c):
                b, g = U // UNITS // TB, U % UNITS
                pe.wait_ge(exp_ok, 5 * U + c + 1)
                if c == 0 and U >= 1:
                    pe.wait_ge(pvout_ok, U)
                if c < 4:
                    nc.tensor.matmul(pv[32 * c:32 * c + 32, :], vmain[:, b, 4 * g + c, :], probs[:, U % 2, c, :],
                                     start=True, stop=False, skip_group_check=True)
                else:
                    nc.tensor.matmul(pv[:, :], vrest[:, b, g, :], probs[:, U % 2, c, :],
                                     start=False, stop=True, skip_group_check=True).then_inc(pv_full, 1)

            for s in STEPS:
                stage, T = s[0], (s[1] if len(s) > 1 else 0)
                if stage == "kv":
                    pe.wait_ge(wkv_in, 16 * 4)
                    for m in range(CC):
                        for k in range(2):
                            last = nc.tensor.matmul(bank("k", m)[:, 0:BATCH * CTX], wkv[0:KD[k], k, m * P:(m + 1) * P],
                                                    ctxT[0:KD[k], k, :], start=(k == 0), stop=(k == 1))
                        fill(last, "k", m)
                    may_fill(pe, "vmain")
                    for b in range(BATCH):
                        for k in range(2):
                            last = nc.tensor.matmul(bank("vmain")[:, b * DIM:(b + 1) * DIM], ctxT[0:KD[k], k, b * CTX:b * CTX + P],
                                                    wkv[0:KD[k], k, DIM:2 * DIM], start=(k == 0), stop=(k == 1))
                    fill(last, "vmain")
                    may_fill(pe, "vrest")
                    for j in range(4):
                        for b in range(BATCH):
                            for k in range(2):
                                w = wkv[0:KD[k], k, DIM:2 * DIM].rearrange("p (g j d) -> p j g d", j=4, d=HD)[:, j]
                                last = nc.tensor.matmul(bank("vrest")[32 * j:32 * j + REST, b * 64:(b + 1) * 64],
                                                        ctxT[0:KD[k], k, b * CTX + P:(b + 1) * CTX], w,
                                                        start=(k == 0), stop=(k == 1))
                    fill(last, "vrest")
                if stage == "q":
                    if T == 0:
                        pe.wait_ge(const_ok, 1)
                        pe.wait_ge(w_in, 16 * 3)
                    pe.wait_ge(xn_ok, T + 1)
                    transposes(xn, "xt", T)
                    for c in range(CC):
                        use = USE[("xt", c, T)]
                        pe.wait_ge(emptied[use % 2], use // 2 + 1)
                    channels("q", wq, xnT, T)
                if stage == "max":
                    if T == 0 and s[2] == 0:
                        pe.wait_ge(kstack_ok, 16 * len(KPARTS))
                        pe.wait_ge(qstack_ok[0], 16 * len(QPARTS))
                    max_scores(T, s[2], range(NG))
                if stage == "maxrows":
                    pe.wait_ge(mparts_ok, T + 1)
                    may_fill(pe, "maxt", T)
                    for t in range(SUB):
                        last = nc.tensor.transpose(bank("maxt", T).bitcast(BF16)[0:3 * HEADS, t * P:(t + 1) * P],
                                                   mparts[:, t, :, :].rearrange("p a h -> p (a h)"), identb[:, :])
                    fill(last, "maxt", T)
                if stage == "attn":
                    i, u = s[1:]
                    U = i * UNITS + u
                    if u == 0:
                        pe.wait_ge(mrows_ok[i % 2], 48 * (i // 2 + 1))
                    if U == 0:
                        pe.wait_ge(v_ok, 1)
                        pe.wait_ge(ones_ok, 1)
                    if u == 0 and i + 1 < TILES:
                        pe.wait_ge(qstack_ok[(i + 1) % 2], 16 * len(QPARTS) * ((i + 1) // 2 + 1))
                    for c in range(5):
                        n = 5 * U + c
                        if n >= 3:
                            pe.wait_ge(exp_ok, n - 2)
                        if c < 4:
                            nc.tensor.matmul(sexp[n % 3][:, :], kstack[:, 4 * u + c, i // TB, 0:P],
                                             qstack[:, i % 2, 4 * u + c, :], start=True, stop=True).then_inc(sexp_full, 1)
                        else:
                            for j in range(4):
                                last = nc.tensor.matmul(sexp[n % 3][32 * j:32 * j + 32, :],
                                                        kstack[:, 4 * u + j, i // TB, P:CPAD],
                                                        qstack[:, i % 2, 4 * u + j, :], start=True, stop=True)
                            last.then_inc(sexp_full, 1)
                        if U >= 1:
                            values(U - 1, c)
                        if i + 1 < TILES:
                            max_scores(i + 1, u, (c,) if c < 4 else (4, 5))
                if stage == "flush":
                    for c in range(5):
                        values(TILES * UNITS - 1, c)
                if stage == "proj":
                    if T == 0:
                        pe.wait_ge(wlate_in, 16 * 5)
                    pe.wait_ge(attn_ok, T + 1)
                    natural("proj", attn, wp, T)
                if stage == "ln2t":
                    pe.wait_ge(xn2_ok, T + 1)
                    transposes(xn2, "x2t", T)
                if stage == "mix":
                    pe.wait_ge(mixed_ok, CC * (T + 1))
                    channels("key", wk, xk, T)
                    natural("gate", xr, wr, T)
                if stage == "out":
                    pe.wait_ge(kact_ok, CC * (T + 1))
                    natural("val", kact, wv, T)


def kernel(x, ctx_768, L0_xattn_q_w, L0_xattn_q_b, L0_xattn_kv_w, L0_xattn_kv_b, L0_xattn_proj_w, L0_xattn_proj_b,
           L0_ffn_W_r, L0_ffn_W_k, L0_ffn_W_v, L0_ffn_mu_r, L0_ffn_mu_k):
    import numpy as _np
    import concourse.bacc as _bacc
    from concourse import mybir as _mybir
    from concourse.bass_utils import run_bass_kernel_spmd as _run

    ctx = _np.asarray(ctx_768)
    laid = {
        "x": _np.asarray(x),
        "ctx_t": ctx.reshape(-1, ctx.shape[-1]).T,
        "q_w": _np.asarray(L0_xattn_q_w),
        "vecs": _np.stack([_np.asarray(L0_xattn_q_b), _np.asarray(L0_xattn_kv_b)[:DIM], _np.asarray(L0_ffn_mu_r),
                           _np.asarray(L0_ffn_mu_k)]).reshape(4, CC, P).transpose(2, 0, 1),
        "kv_w": _np.asarray(L0_xattn_kv_w), "kv_b": _np.asarray(L0_xattn_kv_b),
        "proj_w": _np.asarray(L0_xattn_proj_w), "proj_b": _np.asarray(L0_xattn_proj_b),
        "wr_t": _np.asarray(L0_ffn_W_r).T, "wk_t": _np.asarray(L0_ffn_W_k).T, "wv_t": _np.asarray(L0_ffn_W_v).T,
    }
    nc = _bacc.Bacc("TRN2", target_bir_lowering=False, num_devices=1)
    arrays, args = {}, []
    for name, a in laid.items():
        a = _np.ascontiguousarray(a)
        arrays[f"in_{name}"] = a
        args.append(nc.dram_tensor(f"in_{name}", a.shape, _mybir.dt.from_np(a.dtype), kind="ExternalInput").ap())
    args.append(nc.dram_tensor("out_y", (BATCH, SEQ, DIM), _mybir.dt.float32, kind="ExternalOutput").ap())
    build(nc, *args)
    r = _run(nc, [arrays], core_ids=[0])
    return r.results[0]["out_y"]
```

```python
from contextlib import ExitStack

import concourse.bass as bass
import concourse.mybir as mybir

F32 = mybir.dt.float32
BF16 = mybir.dt.bfloat16
ALU = mybir.AluOpType
ACT = mybir.ActivationFunctionType
AX_X = mybir.AxisListType.X

P = 128
BATCH, SEQ, DIM = 2, 1024, 256
CTX, CDIM = 154, 192
HEADS, HD = 16, 16
TILE = 256
TILES = BATCH * SEQ // TILE
TB = SEQ // TILE
SUB = TILE // P
CC = DIM // P
REST = CTX - P
CPAD = P + 32
QPARTS = (0, 0, 0, 1, 1, 2)
KPARTS = (0, 1, 2, 0, 1, 0)
STACK = 16 * len(QPARTS)
DEPTH = STACK + 3
HH = HEADS // 2
UNITS = HEADS // 4
CHUNKS = 5
RESTS = 2
QBUFS = 3
MAX_BANKS, EXP_BANKS = 2, 3
GROUPS = ((0, 3), (3, 3), (6, 2), (8, 3), (11, 3), (14, 2))
NG = len(GROUPS)
MAXES = SUB * NG
KD = (P, CDIM - P)
TWO_ONES = 1.0019378662109375
EPS = 1e-5
QSCALE = HD ** -0.5


PLACES = {
    ("ln_stats", 0): -2.014, ("ln_scale", 0): -1.953, ("xt",): -1.754, ("q",): -1.701, ("qsplit",): -1.6,
    ("qload",): -1.208, ("max", 0): -0.994, ("max", 1): -0.913, ("max", 2): -0.875, ("max", 3): -0.749, ("max", 4): -0.747,
    ("max", 5): -0.697, ("max", 6): -0.629, ("maxsplit", 0): -0.569, ("max", 7): -0.547, ("max", 8): -0.468,
    ("max", 9): -0.318, ("max", 10): -0.248, ("maxrows", 0): -0.179, ("max", 11): -0.034, ("score", 0, 0): 0.052,
    ("maxsplit", 1): 0.134, ("score", 1, 0): 0.162, ("score", 2, 0): 0.193, ("score", 3, 0): 0.235, ("values", 0, 0): 0.258,
    ("maxrows", 1): 0.263, ("score", 4, 0): 0.364, ("score", 0, 1): 0.452, ("score", 1, 1): 0.499, ("score", 2, 1): 0.518,
    ("score", 3, 1): 0.607, ("values", 1, 0): 0.735, ("numerators", 0): 0.761, ("score", 4, 1): 0.891,
    ("values", 0, 1): 0.939, ("nload", 0): 1.1, ("values", 1, 1): 1.112, ("numerators", 1): 1.149, ("sums",): 1.227,
    ("nload", 1): 1.235, ("resid",): 1.236, ("recip",): 1.289, ("rload",): 1.317, ("scale",): 1.594, ("proj",): 1.838,
    ("ln_stats", 1): 1.842, ("ln_scale", 1): 1.94, ("x2t",): 2.086, ("diff",): 2.129, ("mixed",): 2.225, ("key",): 2.393,
    ("gate",): 2.426, ("val",): 2.905, ("out",): 3.24,
}
SETUPS = ("identity", "k_pad", "v_ones", "k0_rows", "q_rows0", "identity_b", "q_rows1", "k_rows", "q_rows2", "first_token")
OWN_PLACES = {
    ("setup", 0): -3.142, ("ln_stats", 0, 0): -3.096, ("warm", 10, 0): -3.034, ("setup", 1): -3.02,
    ("ln_scale", 0, 0): -2.996, ("k", 0): -2.982, ("xt", 0): -2.976, ("q", 0): -2.975, ("ln_stats", 0, 1): -2.959,
    ("ksplit", 0): -2.951, ("ln_scale", 0, 1): -2.949, ("qsplit", 0): -2.931, ("setup", 2): -2.92, ("xt", 1): -2.919,
    ("setup", 3): -2.911, ("kload", 0): -2.9, ("q", 1): -2.896, ("setup", 4): -2.87, ("qload", 0): -2.866,
    ("setup", 5): -2.851, ("setup", 6): -2.82, ("setup", 7): -2.806, ("setup", 8): -2.784, ("xload", 3): -2.629,
    ("qsplit", 1): -2.594, ("setup", 9): -2.547, ("v", 0): -2.526, ("warm", 1, 0): -2.389, ("warm", 2, 0): -2.335,
    ("kload2", 0): -2.257, ("warm", 3, 0): -2.112, ("xload", 4): 0.011, ("wload", 0): 0.154, ("xload", 5): 0.197,
    ("max", 2, 1): 0.198, ("score", 2, 0, 0): 0.256, ("score", 3, 0, 0): 0.266, ("xload", 6): 0.267, ("q", 2): 0.273,
    ("maxrows", 1, 0): 0.285, ("values", 0, 0, 0): 0.394, ("xload", 7): 0.402, ("qload", 2): 0.616, ("max", 9, 1): 0.738,
    ("wscale", 0): 0.912, ("values", 1, 1, 0): 1.08, ("max", 2, 2): 1.24, ("score", 3, 0, 1): 1.262,
    ("values", 1, 1, 1): 2.06, ("xt", 7): 5.187, ("q", 7): 5.248, ("max", 11, 6): 5.828, ("maxrows", 1, 7): 7.228,
    ("score", 0, 1, 7): 7.424, ("ln_stats", 1, 6): 7.857, ("direct", 0, 7): 8.18, ("direct", 1, 7): 8.287,
    ("warm", 5, 7): 8.985, ("warm", 4, 7): 9.203,
}


def schedule():
    placed = {step + (T,): T + offset for step, offset in PLACES.items() for T in range(TILES)}
    placed.update(OWN_PLACES)
    for step in ("sums", "recip", "rload", "scale"):
        placed.pop((step, TILES - 1))
    return sorted(placed, key=lambda step: placed[step])


def shared_bank_uses(steps):
    number = {}
    for s in steps:
        uses = {"k": [("k", 0), ("k", 1)], "v": [("vmain",), ("vrest",)]}.get(s[0], [s])
        if s[0] in ("k", "v", "xt", "q", "maxrows", "proj", "x2t", "key", "gate", "val"):
            for use in uses:
                number[use] = len(number)
    return number


def build(nc, x, ctx_t, q_w, vecs, kv_w, kv_b, proj_w, proj_b, wr_t, wk_t, wv_t, out):
    STEPS = schedule()
    USE = shared_bank_uses(STEPS)

    with ExitStack() as stack:
        def sb(name, shape, dt=F32):
            return stack.enter_context(nc.sbuf_tensor(name, shape, dt))

        def ps(name, shape, dt=F32):
            return stack.enter_context(nc.psum_tensor(name, shape, dt))

        def sem(name):
            return stack.enter_context(nc.semaphore(name))

        x_nat = sb("x_nat", [P, TILES, SUB, DIM])
        xn = sb("xn", [P, SUB, DIM])
        xnT = sb("xnT", [P, CC, TILE])
        wq = sb("wq", [P, CC, DIM])
        wkv = sb("wkv", [P, 2, 2 * DIM])
        wp = sb("wp", [P, CC, DIM])
        wr = sb("wr", [P, CC, DIM])
        wk = sb("wk", [P, CC, DIM])
        wv = sb("wv", [P, CC, DIM])
        ctxT = sb("ctxT", [P, 2, BATCH * CTX])
        cols = sb("cols", [P, 5, CC])
        vbias = sb("vbias", [P, DIM])
        pbias = sb("pbias", [P, DIM])
        ident = sb("ident", [P, P])
        identb = sb("identb", [P, P], BF16)
        stats = sb("stats", [P, SUB, 6])
        mv = sb("mv", [P, 2, SUB, 2])
        vare = sb("vare", [P, 2, SUB])
        rstd = sb("rstd", [P, 2, SUB])
        warm = sb("warm", [P, 1])
        halves = sb("halves", [P, SUB])
        kf = sb("kf", [P, CC, BATCH * CTX])
        kr = sb("kr", [P, CC, BATCH * CTX])
        kparts = sb("kparts", [P, 3, CC, BATCH, CPAD], BF16)
        qf = sb("qf", [P, CC, TILE])
        qr = sb("qr", [P, CC, TILE])
        qparts = sb("qparts", [P, 3, CC, TILE], BF16)
        kstack = sb("kstack", [P, HEADS, BATCH, CPAD], BF16)
        kstack0 = sb("kstack0", [P, HEADS, BATCH, CPAD], BF16)
        qstack = sb("qstack", [P, QBUFS, HEADS, TILE], BF16)
        vmain = sb("vmain", [P, BATCH, HEADS, 32])
        vrest = sb("vrest", [P, BATCH, UNITS, P])
        nmax = sb("nmax", [P, SUB, HEADS])
        nmaxr = sb("nmaxr", [P, SUB, HEADS])
        mparts = sb("mparts", [P, 2, SUB, 3, HH], BF16)
        mT = sb("mT", [3 * HH, 2, TILE], BF16)
        probs = sb("probs", [P, 2, CHUNKS, 2, TILE])
        pvout = sb("pvout", [P, 2, 2, TILE])
        sums = sb("sums", [P, HEADS * TILE // P])
        rsums = sb("rsums", [P, HEADS * TILE // P])
        attn = sb("attn", [P, 2, CC, TILE])
        rbc = sb("rbc", [P, CC, TILE])
        lsum = sb("lsum", [P, CC, TILE])
        lrec = sb("lrec", [P, CC, TILE])
        xn2 = sb("xn2", [P, SUB, DIM])
        zeros = sb("zeros", [P, 512], BF16)
        x2 = sb("x2", [P, 2, SUB, DIM])
        xn2T = sb("xn2T", [P, 2, CC, TILE + 1])
        diff = sb("diff", [P, CC, TILE])
        xr = sb("xr", [P, CC, TILE])
        xk = sb("xk", [P, CC, TILE])
        kact = sb("kact", [P, CC, TILE])
        gate = sb("gate", [P, SUB, DIM])
        y = sb("y", [P, SUB, DIM])
        relu = diff

        kd = nc.dram_tensor("k_parts_d", [3, HD, HEADS, BATCH * CPAD], BF16, kind="Internal").ap()
        qd = nc.dram_tensor("q_parts_d", [2, 3, HD, HEADS, TILE], BF16, kind="Internal").ap()
        pvd = nc.dram_tensor("pv_d", [2, HEADS, 32, TILE], F32, kind="Internal").ap()
        rsd = nc.dram_tensor("rsums_d", [2, HEADS, TILE], F32, kind="Internal").ap()

        shared = [ps(f"shared{n}", [P, 512]) for n in range(2)]
        smax = [ps(f"smax{n}", [P, 512]) for n in range(MAX_BANKS)]
        sexp = [ps(f"sexp{n}", [P, 512]) for n in range(EXP_BANKS)]
        pv = ps("pv", [P, 512])

        x_in = [sem(f"x_in{t}") for t in range(TILES)]
        cols_in = sem("cols_in")
        wq_in = sem("wq_in")
        vbias_in = sem("vbias_in")
        wkv_in = sem("wkv_in")
        wlate_in = sem("wlate_in")
        setup_ok = sem("setup_ok")
        filled = [sem(f"filled{n}") for n in range(2)]
        emptied = [sem(f"emptied{n}") for n in range(2)]
        v_step = sem("v_step")
        g_step = sem("g_step")
        a_step = sem("a_step")
        var_ok = sem("var_ok")
        rstd_ok = sem("rstd_ok")
        xn_ok = sem("xn_ok")
        xnT_ok = sem("xnT_ok")
        qf_ok = sem("qf_ok")
        kf_ok = sem("kf_ok")
        kparts_ok = sem("kparts_ok")
        kd_ok = sem("kd_ok")
        kstack0_ok = sem("kstack0_ok")
        kstack_ok = sem("kstack_ok")
        v_ok = sem("v_ok")
        qparts_ok = sem("qparts_ok")
        qd_ok = sem("qd_ok")
        qstack_ok = [sem(f"qstack_ok{n}") for n in range(QBUFS)]
        smax_full = sem("smax_full")
        smax_read = sem("smax_read")
        mparts_ok = sem("mparts_ok")
        mT_ok = sem("mT_ok")
        mrows_ok = [sem(f"mrows_ok{n}") for n in range(2)]
        sexp_full = sem("sexp_full")
        exp_ok = sem("exp_ok")
        pv_full = sem("pv_full")
        pvout_ok = sem("pvout_ok")
        pvd_ok = [sem(f"pvd_ok{n}") for n in range(2)]
        lsum_in = [sem(f"lsum_in{n}") for n in range(2)]
        sums_ok = [sem(f"sums_ok{n}") for n in range(2)]
        zeros_ok = sem("zeros_ok")
        rsums_ok = sem("rsums_ok")
        rsd_ok = [sem(f"rsd_ok{n}") for n in range(2)]
        rbc_ok = [sem(f"rbc_ok{n}") for n in range(2)]
        attn_in = [[sem(f"attn_in{n}_{half}") for half in range(2)] for n in range(2)]
        attn_ok = sem("attn_ok")
        x2_ok = sem("x2_ok")
        resid_ok = sem("resid_ok")
        xn2_ok = sem("xn2_ok")
        xn2T_ok = sem("xn2T_ok")
        diff_ok = sem("diff_ok")
        mixed_ok = sem("mixed_ok")
        kact_ok = sem("kact_ok")
        gate_ok = sem("gate_ok")
        wv_ok = sem("wv_ok")
        gated_ok = sem("gated_ok")
        y_ok = sem("y_ok")
        y_out = sem("y_out")

        x_d = x.rearrange("b (t s p) c -> (b t) p s c", s=SUB, p=P)
        out_d = out.rearrange("b (t s p) c -> (b t) p s c", s=SUB, p=P)

        def maximum(n):
            half = n // (MAXES // 2)
            return half, n % (MAXES // 2) // (NG // 2), half * (NG // 2) + n % (NG // 2)

        def bank(*use):
            return shared[USE[use] % 2]

        def may_fill(eng, *use):
            n = USE[use]
            if n >= 2:
                eng.wait_ge(emptied[n % 2], n // 2)

        def fill(ins, *use):
            ins.then_inc(filled[USE[use] % 2], 1)

        def await_bank(eng, *use):
            n = USE[use]
            eng.wait_ge(filled[n % 2], n // 2 + 1)

        def empty(ins, *use):
            ins.then_inc(emptied[USE[use] % 2], 1)

        def last_token(T):
            return xn2T[:, T % 2, :, 0:1], xn2T[:, (T - 1) % 2, :, TILE:TILE + 1]

        def difference(T, c):
            return diff[:, c, :], xn2T[:, T % 2, c, 1:TILE + 1], xn2T[:, T % 2, c, 0:TILE]

        def await_setup(eng, name):
            eng.wait_ge(setup_ok, SETUPS.index(name) + 1)

        block = stack.enter_context(nc.Block())

        @block.sync
        def _(sp):
            sp.dma_start(x_nat[:, 0], x_d[0]).then_inc(x_in[0], 16)
            for k in range(2):
                sp.dma_start(ctxT[0:KD[k], k, :], ctx_t[k * P:k * P + KD[k], :]).then_inc(wkv_in, 16)
                sp.dma_start(wkv[0:KD[k], k, :], kv_w[k * P:k * P + KD[k], :]).then_inc(wkv_in, 16)
            sp.dma_start(cols[:, 0:4, :], vecs).then_inc(cols_in, 16)
            sp.dma_start(wq[:, :, :], q_w.rearrange("(c p) n -> p c n", p=P)).then_inc(wq_in, 16)
            sp.dma_start(x_nat[:, 1], x_d[1]).then_inc(x_in[1], 16)
            sp.dma_start(vbias[:, :], kv_b[DIM:2 * DIM].partition_broadcast(P)).then_inc(vbias_in, 16)
            sp.dma_start(x_nat[:, 2], x_d[2]).then_inc(x_in[2], 16)

            def load_k(target, loaded):
                for n, parts in ((0, 3), (3, 2), (5, 1)):
                    sp.dma_start(target[HD * n:HD * (n + parts), :, :, :].rearrange("p h b n -> p (h b n)"),
                                 kd[0:parts].rearrange("a d h n -> (a d) (h n)")).then_inc(loaded, 16)

            for s in STEPS:
                stage, T = s[0], s[-1]
                if stage == "ksplit":
                    sp.wait_ge(kparts_ok, 1)
                    sp.dma_start(kd.rearrange("a (m d) h n -> (d h) (a m) n", m=CC),
                                 kparts[:, :, :, :, :].rearrange("p a m b n -> p (a m) (b n)")).then_inc(kd_ok, 16)
                if stage == "kload":
                    sp.wait_ge(kd_ok, 16)
                    load_k(kstack0, kstack0_ok)
                if stage == "qsplit":
                    sp.wait_ge(qparts_ok, T + 1)
                    sp.dma_start(qd[T % 2].rearrange("a (m d) h n -> (d h) (a m) n", m=CC), qparts[:, :, :, :].rearrange("p a m n -> p (a m) n")).then_inc(qd_ok, 16)
                if stage == "qload":
                    sp.wait_ge(qd_ok, 16 * (T + 1))
                    if T >= QBUFS:
                        sp.wait_ge(sexp_full, 2 * CHUNKS * (T - QBUFS + 1))
                    for part, (n, copies) in enumerate(((0, 3), (3, 2), (5, 1))):
                        sp.dma_start(qstack[HD * n:HD * (n + copies), T % QBUFS, :, :].rearrange("p h n -> p (h n)"),
                                     qd[T % 2, part:part + 1].rearrange("a d h n -> a d (h n)").to_broadcast([copies, HD, HEADS * TILE])
                                     ).then_inc(qstack_ok[T % QBUFS], 16)
                if stage == "kload2":
                    load_k(kstack, kstack_ok)
                if stage == "xload":
                    sp.dma_start(x_nat[:, T], x_d[T]).then_inc(x_in[T], 16)
                if stage == "wload":
                    for w_sb, w_d in ((wp, proj_w), (wr, wr_t), (wk, wk_t), (wv, wv_t)):
                        sp.dma_start(w_sb[:, :, :], w_d.rearrange("(c p) n -> p c n", p=P)).then_inc(wlate_in, 16)
                    sp.dma_start(pbias[:, :], proj_b.partition_broadcast(P)).then_inc(wlate_in, 16)
                if stage == "maxrows":
                    half = s[1]
                    sp.wait_ge(mT_ok, 2 * T + half + 1)
                    if T < QBUFS:
                        await_setup(sp, f"q_rows{T}")
                    sp.dma_start(qstack[STACK:DEPTH, T % QBUFS, HH * half:HH * (half + 1), :], mT[:, half, :]).then_inc(mrows_ok[half], 16)
                if stage == "numerators":
                    half = s[1]
                    sp.wait_ge(pvout_ok, 2 * T + half + 1)
                    sp.dma_start(pvd[T % 2, HH * half:HH * (half + 1)].rearrange("(u h) r n -> (h r) u n", u=2),
                                 pvout[:, half, :, :]).then_inc(pvd_ok[half], 16)
                if stage == "nload":
                    half = s[1]
                    sp.wait_ge(pvd_ok[half], 16 * (T + 1))
                    if T == TILES - 1:
                        sp.dma_start(lsum[:, half, :], pvd[T % 2, HH * half:HH * (half + 1), HD:2 * HD, :]).then_inc(lsum_in[half], 16)
                    if T >= 2:
                        await_bank(sp, "proj", T - 2)
                    sp.dma_start(attn[:, T % 2, half, :], pvd[T % 2, HH * half:HH * (half + 1), 0:HD, :]).then_inc(attn_in[T % 2][half], 16)
                if stage == "sums":
                    for n in range(2):
                        sp.wait_ge(pvd_ok[n], 16 * (T + 1))
                    if T >= 1:
                        sp.wait_ge(rsums_ok, T)
                    sp.dma_start(sums[:, :], pvd[T % 2, :, HD, :].rearrange("h (c n) -> h c n", n=HEADS * TILE // P)).then_inc(sums_ok[T % 2], 16)
                if stage == "recip":
                    sp.wait_ge(rsums_ok, T + 1)
                    sp.dma_start(rsd[T % 2].rearrange("h (c n) -> h c n", n=HEADS * TILE // P), rsums[:, :]).then_inc(rsd_ok[T % 2], 16)
                if stage == "rload":
                    sp.wait_ge(rsd_ok[T % 2], 16 * (T // 2 + 1))
                    if T >= 1:
                        sp.wait_ge(attn_ok, T)
                    for c in range(CC):
                        sp.dma_start(rbc[:, c, :],
                                     rsd[T % 2, 8 * c:8 * c + 8, :].rearrange("h (o n) -> h o n", o=1).to_broadcast([8, HD, TILE])
                                     ).then_inc(rbc_ok[T % 2], 16)
                if stage == "out":
                    sp.wait_ge(y_ok, T + 1)
                    sp.dma_start(out_d[T], y[:, :, :]).then_inc(y_out, 16)
            sp.wait_ge(y_out, 16 * TILES)

        @block.gpsimd
        def _(pool):
            steps = [0]

            def step(ins):
                ins.then_inc(g_step, 1)
                steps[0] += 1
                pool.wait_ge(g_step, steps[0])

            norms = [0]

            def identity(t):
                step(nc.gpsimd.memset(t[:, :], 0.0))
                step(nc.gpsimd.affine_select(out=t[:, :], in_=t[:, :], compare_op=ALU.not_equal, fill=1.0,
                                             base=0, pattern=[[-1, P]], channel_multiplier=1))

            def setup(name):
                if norms[0]:
                    pool.wait_ge(rstd_ok, norms[0])
                if name == "identity":
                    identity(ident)
                if name == "identity_b":
                    identity(identb)
                if name == "k_pad":
                    step(nc.gpsimd.memset(kparts[:, :, :, :, CTX:CPAD], 0.0))
                if name in ("k0_rows", "k_rows"):
                    t = kstack if name == "k_rows" else kstack0
                    step(nc.gpsimd.memset(t[STACK:P].rearrange("p h b n -> p (h b n)").bitcast(F32), 0.0))
                if name == "k_rows":
                    ones = kstack[STACK:DEPTH, :, :, :].rearrange("p h b n -> p (h b) n").bitcast(F32)
                    step(nc.gpsimd.memset(ones[:, :, 0:CTX // 2], TWO_ONES))
                if name[:-1] == "q_rows":
                    step(nc.gpsimd.memset(qstack[STACK:P, int(name[-1])].rearrange("p h n -> p (h n)").bitcast(F32), 0.0))
                if name == "v_ones":
                    nc.gpsimd.memset(vmain[:, :, :, HD:32], 1.0)
                    step(nc.gpsimd.memset(vrest[:, :, :, :], 0.0))
                    for j in range(4):
                        step(nc.gpsimd.memset(vrest[32 * j:32 * j + REST, :, :, 32 * j + HD:32 * j + 32], 1.0))
                if name == "first_token":
                    step(nc.gpsimd.memset(xn2T[:, 0, :, 0:1], 0.0))
                pool.sem_inc(setup_ok, 1)

            step(nc.gpsimd.memset(halves[:, :], -0.5))
            for s in STEPS:
                stage, T = s[0], s[-1]
                if stage == "ln_stats":
                    which = s[1]
                    norms[0] += 1
                    pool.wait_ge(var_ok, norms[0])
                    nc.gpsimd.tensor_tensor(rstd[:, which, :], vare[:, which, :], halves[:, :], ALU.pow).then_inc(rstd_ok, 1)
                if stage == "setup":
                    setup(SETUPS[s[1]])
                if stage == "resid":
                    pool.wait_ge(xn_ok, T + 1)
                    if T == 0:
                        pool.wait_ge(wlate_in, 16 * 5)
                    for t in range(SUB):
                        last = nc.gpsimd.tensor_tensor(x_nat[:, T, t, :], x_nat[:, T, t, :], pbias[:, :], ALU.add)
                    last.then_inc(resid_ok, 1)
                if stage == "out" and T < TILES - 1:
                    pool.wait_ge(gated_ok, T + 1)
                    if T >= 1:
                        pool.wait_ge(y_out, 16 * T)
                    for t in range(SUB):
                        last = nc.gpsimd.tensor_tensor(y[:, t, :], gate[:, t, :], x2[:, T % 2, t, :], ALU.add)
                    last.then_inc(y_ok, 1)
                if stage == "diff" and T < TILES - 1:
                    pool.wait_ge(xn2T_ok, T + 1)
                    if T >= 1:
                        pool.wait_ge(kact_ok, T)
                    if T % TB:
                        step(nc.gpsimd.tensor_copy(*last_token(T)))
                    elif T:
                        step(nc.gpsimd.memset(xn2T[:, T % 2, :, 0:1], 0.0))
                    for c in range(CC):
                        nc.gpsimd.tensor_tensor(*difference(T, c), ALU.subtract).then_inc(diff_ok, 1)

        @block.scalar
        def _(act):
            act.wait_ge(g_step, 1)
            nc.scalar.activation(warm[:, :], halves[:, 0:1], ACT.Exp)
            for s in STEPS:
                stage, T = s[0], s[-1]
                if stage == "k":
                    act.wait_ge(cols_in, 16)
                    for m in range(CC):
                        await_bank(act, "k", m)
                        empty(nc.scalar.activation(kf[:, m, :], bank("k", m)[:, 0:BATCH * CTX], ACT.Identity,
                                                   bias=cols[:, 1, m:m + 1]), "k", m)
                if stage == "xt":
                    await_bank(act, *s)
                    if T >= 1:
                        await_bank(act, "q", T - 1)
                    empty(nc.scalar.copy(xnT[:, :, :].rearrange("p c n -> p (c n)"), bank(*s)[:, :]), *s)
                if stage == "q":
                    if T == 0:
                        act.wait_ge(a_step, 1)
                    await_bank(act, *s)
                    if T >= 1:
                        act.wait_ge(qd_ok, 16 * T)
                    for target in (qf, qparts[:, 0]):
                        for m in range(CC):
                            last = nc.scalar.activation(target[:, m, :], bank(*s)[:, m * TILE:(m + 1) * TILE], ACT.Identity,
                                                        bias=cols[:, 4, m:m + 1], scale=QSCALE)
                    empty(last, *s)
                if stage == "maxrows":
                    half = s[1]
                    await_bank(act, *s)
                    if T >= 1:
                        act.wait_ge(mrows_ok[half], 16 * T)
                    nc.scalar.copy(mT[:, half, :], bank(*s).bitcast(BF16)[0:3 * HH, 0:TILE]).then_inc(mT_ok, 1)
                    act.wait_ge(mT_ok, 2 * T + half + 1)
                    act.sem_inc(emptied[USE[s] % 2], 1)
                if stage == "score":
                    c, half = s[1:3]
                    H = 2 * T + half
                    n = CHUNKS * H + c
                    act.wait_ge(sexp_full, n + 1)
                    if T >= 1 and c == 0:
                        act.wait_ge(pv_full, H - 1)
                    nc.scalar.activation(probs[:, half, c, :, :].rearrange("p a n -> p (a n)"), sexp[n % EXP_BANKS][:, :],
                                         ACT.Exp).then_inc(exp_ok, 1)
                if stage == "numerators":
                    half = s[1]
                    H = 2 * T + half
                    act.wait_ge(pv_full, H + 1)
                    if T >= 1:
                        act.wait_ge(pvd_ok[half], 16 * T)
                    nc.scalar.copy(pvout[:, half, :, :].rearrange("p u n -> p (u n)"), pv[:, :]).then_inc(pvout_ok, 1)
                if stage == "x2t":
                    await_bank(act, *s)
                    if T >= 2:
                        act.wait_ge(mixed_ok, 2 * (T - 1))
                        act.wait_ge(diff_ok, CC * T)
                    nc.scalar.copy(xn2T[:, T % 2, :, 1:TILE + 1],
                                   bank(*s)[:, :].rearrange("p (c n) -> p c n", c=CC)).then_inc(xn2T_ok, 1)
                    act.wait_ge(xn2T_ok, T + 1)
                    act.sem_inc(emptied[USE[s] % 2], 1)
                if stage == "key":
                    await_bank(act, *s)
                    act.wait_ge(mixed_ok, 2 * (T + 1))
                    empty(nc.scalar.activation(relu[:, :, :].rearrange("p c n -> p (c n)"), bank(*s)[:, :], ACT.Relu), *s)
                    act.wait_ge(emptied[USE[s] % 2], USE[s] // 2 + 1)
                    if T >= 1:
                        act.wait_ge(y_ok, T)
                    nc.scalar.activation(kact[:, :, :], relu[:, :, :], ACT.Square).then_inc(kact_ok, 1)
                if stage == "gate":
                    await_bank(act, *s)
                    empty(nc.scalar.activation(gate[:, :, :].rearrange("p s c -> p (s c)"), bank(*s)[:, :], ACT.Tanh, scale=0.5), *s)

        @block.vector
        def _(dve):
            steps = [0]

            def step(ins):
                ins.then_inc(v_step, 1)
                steps[0] += 1
                dve.wait_ge(v_step, steps[0])

            norms = [0]
            nc.vector.memset(zeros[:, :], 0.0).then_inc(zeros_ok, 1)

            def split(whole, left, parts):
                step(nc.vector.tensor_copy(parts[0], whole))
                return split_rest(whole, left, parts)

            def split_rest(whole, left, parts):
                step(nc.vector.tensor_tensor(left, whole, parts[0], ALU.subtract))
                step(nc.vector.tensor_copy(parts[1], left))
                return nc.vector.tensor_tensor(parts[2], left, parts[1], ALU.subtract)

            def read(use):
                dve.wait_ge(emptied[USE[use] % 2], USE[use] // 2 + 1)

            for s in STEPS:
                stage, T = s[0], s[-1]
                if stage == "ln_stats":
                    which = s[1]
                    source = x_nat[:, T] if which == 0 else x2[:, T % 2]
                    if which == 0:
                        dve.wait_ge(x_in[T], 16)
                    for t in range(SUB):
                        last = nc.vector.bn_stats(out=stats[:, t, :], in_=source[:, t, :])
                    step(last)
                    for t in range(SUB):
                        last = nc.vector.bn_aggr(out=mv[:, which, t, :], in_=stats[:, t, :])
                    step(last)
                    nc.vector.tensor_scalar_add(vare[:, which, :], mv[:, which, :, 1], EPS).then_inc(var_ok, 1)
                if stage == "ln_scale":
                    which = s[1]
                    source = x_nat[:, T] if which == 0 else x2[:, T % 2]
                    target = xn if which == 0 else xn2
                    if which == 0 and T >= 1:
                        await_bank(dve, "xt", T - 1)
                    norms[0] += 1
                    dve.wait_ge(rstd_ok, norms[0])
                    for t in range(SUB):
                        last = nc.vector.tensor_scalar(target[:, t, :], source[:, t, :], mv[:, which, t, 0:1],
                                                       rstd[:, which, t:t + 1], ALU.subtract, ALU.mult)
                    last.then_inc(xn_ok if which == 0 else xn2_ok, 1)
                if stage == "k":
                    dve.wait_ge(cols_in, 16)
                    nc.vector.tensor_scalar_mul(cols[:, 4, :], cols[:, 0, :], QSCALE).then_inc(a_step, 1)
                if stage == "ksplit":
                    for m in range(CC):
                        read(("k", m))
                    await_setup(dve, "k_pad")
                    split(kf[:, :, :].rearrange("p m (b n) -> p m b n", b=BATCH),
                          kr[:, :, :].rearrange("p m (b n) -> p m b n", b=BATCH),
                          [kparts[:, a, :, :, 0:CTX] for a in range(3)]).then_inc(kparts_ok, 1)
                if stage == "v":
                    dve.wait_ge(vbias_in, 16)
                    await_bank(dve, "vmain")
                    for b in range(BATCH):
                        last = nc.vector.tensor_tensor(
                            vmain[:, b, :, 0:HD], bank("vmain")[:, b * DIM:(b + 1) * DIM].rearrange("p (h d) -> p h d", d=HD),
                            vbias[:, :].rearrange("p (h d) -> p h d", d=HD), ALU.add)
                    empty(last, "vmain")
                    await_bank(dve, "vrest")
                    await_setup(dve, "v_ones")
                    for j in range(4):
                        rows = slice(32 * j, 32 * j + REST)
                        for b in range(BATCH):
                            last = nc.vector.tensor_tensor(
                                vrest[rows, b, :, 32 * j:32 * j + HD],
                                bank("vrest")[rows, b * 64:(b + 1) * 64].rearrange("p (g d) -> p g d", d=HD),
                                vbias[rows, :].rearrange("p (g j d) -> p j g d", j=4, d=HD)[:, j], ALU.add)
                    step(last)
                    dve.sem_inc(v_ok, 1)
                    dve.sem_inc(emptied[USE[("vrest",)] % 2], 1)
                if stage == "qsplit":
                    read(("q", T))
                    split_rest(qf[:, :, :], qr[:, :, :], [qparts[:, a, :, :] for a in range(3)]).then_inc(qparts_ok, 1)
                if stage == "max":
                    half, t, g = maximum(s[1])
                    h0, nh = GROUPS[g]
                    n = T * MAXES + s[1]
                    dve.wait_ge(smax_full, n + 1)
                    if T >= 1 and t == 0:
                        dve.wait_ge(mparts_ok, 2 * T - 1 + half)
                    nc.vector.tensor_reduce(nmax[:, t, h0:h0 + nh],
                                            smax[n % MAX_BANKS][:, 0:nh * CTX].rearrange("p (h n) -> p h n", n=CTX),
                                            AX_X, ALU.max, negate=True).then_inc(smax_read, 1)
                if stage == "maxsplit":
                    half = s[1]
                    dve.wait_ge(smax_read, T * MAXES + (half + 1) * MAXES // 2)
                    if T >= 1:
                        await_bank(dve, "maxrows", half, T - 1)
                    hs = slice(HH * half, HH * (half + 1))
                    split(nmax[:, :, hs], nmaxr[:, :, hs], [mparts[:, half, :, a, :] for a in range(3)]).then_inc(mparts_ok, 1)
                if stage == "recip":
                    dve.wait_ge(sums_ok[T % 2], 16 * (T // 2 + 1))
                    if T >= 1:
                        dve.wait_ge(rsd_ok[(T - 1) % 2], 16 * ((T - 1) // 2 + 1))
                    nc.vector.reciprocal(rsums[:, :], sums[:, :]).then_inc(rsums_ok, 1)
                if stage == "scale":
                    for half in range(2):
                        dve.wait_ge(attn_in[T % 2][half], 16 * (T // 2 + 1))
                    dve.wait_ge(rbc_ok[T % 2], 32 * (T // 2 + 1))
                    nc.vector.tensor_tensor(attn[:, T % 2, :, :], attn[:, T % 2, :, :], rbc[:, :, :], ALU.mult).then_inc(attn_ok, 1)
                if stage == "direct":
                    half = s[1]
                    dve.wait_ge(lsum_in[half], 16)
                    step(nc.vector.reciprocal(lrec[:, half, :], lsum[:, half, :]))
                    dve.wait_ge(attn_in[T % 2][half], 16 * (T // 2 + 1))
                    last = nc.vector.tensor_tensor(attn[:, T % 2, half, :], attn[:, T % 2, half, :], lrec[:, half, :], ALU.mult)
                    step(last)
                    if half:
                        dve.sem_inc(attn_ok, 1)
                if stage == "proj":
                    dve.wait_ge(resid_ok, T + 1)
                    if T >= 2:
                        dve.wait_ge(y_ok, T - 1)
                    await_bank(dve, *s)
                    nc.vector.tensor_tensor(x2[:, T % 2, :, :].rearrange("p s c -> p (s c)"), bank(*s)[:, :],
                                            x_nat[:, T, :, :].rearrange("p s c -> p (s c)"), ALU.add).then_inc(x2_ok, 1)
                    dve.wait_ge(x2_ok, T + 1)
                    dve.sem_inc(emptied[USE[s] % 2], 1)
                if stage == "diff" and T == TILES - 1:
                    dve.wait_ge(xn2T_ok, T + 1)
                    dve.wait_ge(kact_ok, T)
                    step(nc.vector.tensor_copy(*last_token(T)))
                    for c in range(CC):
                        nc.vector.tensor_tensor(*difference(T, c), ALU.subtract).then_inc(diff_ok, 1)
                if stage == "mixed":
                    dve.wait_ge(diff_ok, CC * (T + 1))
                    if T >= 1:
                        await_bank(dve, "gate", T - 1)
                    for target, n in ((xk, 3), (xr, 2)):
                        for c in range(CC):
                            last = nc.vector.scalar_tensor_tensor(
                                out=target[:, c, :], in0=diff[:, c, :], scalar=cols[:, n, c:c + 1],
                                in1=xn2T[:, T % 2, c, 0:TILE], op0=ALU.mult, op1=ALU.add)
                        last.then_inc(mixed_ok, 1)
                if stage == "val":
                    read(("gate", T))
                    await_bank(dve, *s)
                    g2 = gate[:, :, :].rearrange("p s c -> p (s c)")
                    nc.vector.scalar_tensor_tensor(out=g2, in0=g2, scalar=1.0, in1=bank(*s)[:, :],
                                                   op0=ALU.add, op1=ALU.mult).then_inc(gated_ok, 1)
                    dve.wait_ge(gated_ok, T + 1)
                    dve.sem_inc(emptied[USE[s] % 2], 1)
                if stage == "out" and T == TILES - 1:
                    dve.wait_ge(y_out, 16 * T)
                    nc.vector.tensor_tensor(y[:, :, :], gate[:, :, :], x2[:, T % 2, :, :], ALU.add).then_inc(y_ok, 1)
                if stage == "wscale":
                    dve.wait_ge(wlate_in, 16 * 5)
                    nc.vector.tensor_scalar_mul(wv[:, :, :], wv[:, :, :], 0.5).then_inc(wv_ok, 1)

        @block.tensor
        def _(pe):
            def transposes(source, *use):
                may_fill(pe, *use)
                for c in range(CC):
                    for t in range(SUB):
                        last = nc.tensor.transpose(bank(*use)[:, c * TILE + t * P:c * TILE + (t + 1) * P],
                                                   source[:, t, c * P:(c + 1) * P], ident[:, :])
                fill(last, *use)

            def natural(lhs, w, *use):
                may_fill(pe, *use)
                for t in range(SUB):
                    for k in range(CC):
                        last = nc.tensor.matmul(bank(*use)[:, t * DIM:(t + 1) * DIM], lhs[:, k, t * P:(t + 1) * P], w[:, k, :],
                                                start=(k == 0), stop=(k == CC - 1))
                fill(last, *use)

            def channels(w, rhs, *use):
                may_fill(pe, *use)
                for m in range(CC):
                    for k in range(CC):
                        last = nc.tensor.matmul(bank(*use)[:, m * TILE:(m + 1) * TILE], w[:, k, m * P:(m + 1) * P], rhs[:, k, :],
                                                start=(k == 0), stop=(k == CC - 1))
                fill(last, *use)

            for s in STEPS:
                stage, T = s[0], s[-1]
                if stage == "warm":
                    pe.wait_ge(zeros_ok, 1)
                    if T == TILES - 1:
                        pe.wait_ge(smax_read, TILES * MAXES)
                    for _ in range(s[1]):
                        nc.tensor.matmul(smax[0][:, :], zeros[:, 0:P], zeros[:, :], start=True, stop=True)
                if stage == "k":
                    pe.wait_ge(wkv_in, 16 * 4)
                    for m in range(CC):
                        for k in range(2):
                            last = nc.tensor.matmul(bank("k", m)[:, 0:BATCH * CTX], wkv[0:KD[k], k, m * P:(m + 1) * P],
                                                    ctxT[0:KD[k], k, :], start=(k == 0), stop=(k == 1))
                        fill(last, "k", m)
                if stage == "v":
                    may_fill(pe, "vmain")
                    for b in range(BATCH):
                        for k in range(2):
                            last = nc.tensor.matmul(bank("vmain")[:, b * DIM:(b + 1) * DIM], ctxT[0:KD[k], k, b * CTX:b * CTX + P],
                                                    wkv[0:KD[k], k, DIM:2 * DIM], start=(k == 0), stop=(k == 1))
                    fill(last, "vmain")
                    may_fill(pe, "vrest")
                    for j in range(4):
                        for b in range(BATCH):
                            for k in range(2):
                                w = wkv[0:KD[k], k, DIM:2 * DIM].rearrange("p (g j d) -> p j g d", j=4, d=HD)[:, j]
                                last = nc.tensor.matmul(bank("vrest")[32 * j:32 * j + REST, b * 64:(b + 1) * 64],
                                                        ctxT[0:KD[k], k, b * CTX + P:(b + 1) * CTX], w,
                                                        start=(k == 0), stop=(k == 1))
                    fill(last, "vrest")
                if stage == "xt":
                    if T == 0:
                        await_setup(pe, "identity")
                    pe.wait_ge(xn_ok, T + 1)
                    transposes(xn, *s)
                if stage == "q":
                    use = USE[("xt", T)]
                    pe.wait_ge(emptied[use % 2], use // 2 + 1)
                    if T == 0:
                        pe.wait_ge(wq_in, 16)
                    channels(wq, xnT, *s)
                if stage == "max":
                    half, t, g = maximum(s[1])
                    h0, nh = GROUPS[g]
                    n = T * MAXES + s[1]
                    if n == 0:
                        pe.wait_ge(kstack0_ok, 16 * 3)
                        await_setup(pe, "k0_rows")
                    if T < QBUFS and s[1] == 0:
                        await_setup(pe, f"q_rows{T}")
                    if s[1] == 0:
                        pe.wait_ge(qstack_ok[T % QBUFS], 16 * 3 * (T // QBUFS + 1))
                    if n >= MAX_BANKS:
                        pe.wait_ge(smax_read, n - MAX_BANKS + 1)
                    for k in range(nh):
                        last = nc.tensor.matmul(smax[n % MAX_BANKS][:, k * CTX:(k + 1) * CTX],
                                                qstack[:, T % QBUFS, h0 + k, t * P:(t + 1) * P],
                                                kstack0[:, h0 + k, T // TB, 0:CTX], start=True, stop=True)
                    last.then_inc(smax_full, 1)
                if stage == "maxrows":
                    half = s[1]
                    pe.wait_ge(mparts_ok, 2 * T + half + 1)
                    if T == 0:
                        await_setup(pe, "identity_b")
                    may_fill(pe, *s)
                    for t in range(SUB):
                        last = nc.tensor.transpose(bank(*s).bitcast(BF16)[0:24, t * P:(t + 1) * P],
                                                   mparts[:, half, t, :, :].rearrange("p a h -> p (a h)"), identb[:, :])
                    fill(last, *s)
                if stage == "score":
                    c, half = s[1:3]
                    if T == 0 and half == 0 and c == 0:
                        pe.wait_ge(kstack_ok, 16 * 3)
                        await_setup(pe, "k_rows")
                    if c == 0:
                        pe.wait_ge(mrows_ok[half], 16 * (T + 1))
                    n = CHUNKS * (2 * T + half) + c
                    if n >= EXP_BANKS:
                        pe.wait_ge(exp_ok, n - EXP_BANKS + 1)
                    for a in range(2):
                        cols_a = slice(a * TILE, (a + 1) * TILE)
                        if c != RESTS:
                            h = HH * half + 2 * (c - (c > RESTS)) + a
                            last = nc.tensor.matmul(sexp[n % EXP_BANKS][:, cols_a], kstack[:, h, T // TB, 0:P], qstack[:, T % QBUFS, h, :],
                                                    start=True, stop=True)
                        else:
                            for j in range(4):
                                h = HH * half + 4 * a + j
                                last = nc.tensor.matmul(sexp[n % EXP_BANKS][32 * j:32 * j + 32, cols_a], kstack[:, h, T // TB, P:CPAD],
                                                        qstack[:, T % QBUFS, h, :], start=True, stop=True)
                    last.then_inc(sexp_full, 1)
                if stage == "values":
                    a, half = s[1:3]
                    H = 2 * T + half
                    if H == 0 and a == 0:
                        pe.wait_ge(v_ok, 1)
                    if H >= 1 and a == 0:
                        pe.wait_ge(pvout_ok, H)
                    pe.wait_ge(exp_ok, CHUNKS * H + (CHUNKS if a else RESTS + 1))
                    unit = slice(a * TILE, (a + 1) * TILE)
                    for j in range(4):
                        nc.tensor.matmul(pv[32 * j:32 * j + 32, unit], vmain[:, T // TB, HH * half + 4 * a + j, :],
                                         probs[:, half, 3 * a + j // 2, j % 2, :], start=True, stop=False, skip_group_check=True)
                    last = nc.tensor.matmul(pv[:, unit], vrest[:, T // TB, 2 * half + a, :], probs[:, half, RESTS, a, :],
                                            start=False, stop=True, skip_group_check=True)
                    if a:
                        last.then_inc(pv_full, 1)
                if stage == "proj":
                    if T == 0:
                        pe.wait_ge(wlate_in, 16 * 5)
                    pe.wait_ge(attn_ok, T + 1)
                    natural(attn[:, T % 2], wp, *s)
                if stage == "x2t":
                    pe.wait_ge(xn2_ok, T + 1)
                    transposes(xn2, *s)
                if stage == "key":
                    pe.wait_ge(mixed_ok, 2 * T + 1)
                    channels(wk, xk, *s)
                if stage == "gate":
                    pe.wait_ge(mixed_ok, 2 * (T + 1))
                    natural(xr, wr, *s)
                if stage == "val":
                    if T == 0:
                        pe.wait_ge(wv_ok, 1)
                    pe.wait_ge(kact_ok, T + 1)
                    natural(kact, wv, *s)


def kernel(x, ctx_768, L0_xattn_q_w, L0_xattn_q_b, L0_xattn_kv_w, L0_xattn_kv_b, L0_xattn_proj_w, L0_xattn_proj_b,
           L0_ffn_W_r, L0_ffn_W_k, L0_ffn_W_v, L0_ffn_mu_r, L0_ffn_mu_k):
    import numpy as _np
    import concourse.bacc as _bacc
    from concourse import mybir as _mybir
    from concourse.bass_utils import run_bass_kernel_spmd as _run

    ctx = _np.asarray(ctx_768)
    kv_w = _np.asarray(L0_xattn_kv_w)

    def by_d(a):
        return _np.swapaxes(a.reshape(a.shape[:-1] + (HEADS, HD)), -1, -2).reshape(a.shape)

    laid = {
        "x": _np.asarray(x),
        "ctx_t": ctx.reshape(-1, ctx.shape[-1]).T,
        "q_w": by_d(_np.asarray(L0_xattn_q_w)),
        "vecs": _np.stack([by_d(_np.asarray(L0_xattn_q_b)), by_d(_np.asarray(L0_xattn_kv_b)[:DIM]), _np.asarray(L0_ffn_mu_r),
                           _np.asarray(L0_ffn_mu_k)]).reshape(4, CC, P).transpose(2, 0, 1),
        "kv_w": _np.concatenate([by_d(kv_w[:, :DIM]), kv_w[:, DIM:]], axis=1), "kv_b": _np.asarray(L0_xattn_kv_b),
        "proj_w": _np.asarray(L0_xattn_proj_w), "proj_b": _np.asarray(L0_xattn_proj_b),
        "wr_t": _np.asarray(L0_ffn_W_r).T, "wk_t": _np.asarray(L0_ffn_W_k).T, "wv_t": _np.asarray(L0_ffn_W_v).T,
    }
    nc = _bacc.Bacc("TRN2", target_bir_lowering=False, num_devices=1)
    arrays, args = {}, []
    for name, a in laid.items():
        a = _np.ascontiguousarray(a)
        arrays[f"in_{name}"] = a
        args.append(nc.dram_tensor(f"in_{name}", a.shape, _mybir.dt.from_np(a.dtype), kind="ExternalInput").ap())
    args.append(nc.dram_tensor("out_y", (BATCH, SEQ, DIM), _mybir.dt.float32, kind="ExternalOutput").ap())
    build(nc, *args)
    r = _run(nc, [arrays], core_ids=[0])
    return r.results[0]["out_y"]
```

```python
from contextlib import ExitStack

import concourse.bass as bass
import concourse.mybir as mybir

F32 = mybir.dt.float32
BF16 = mybir.dt.bfloat16
ALU = mybir.AluOpType
ACT = mybir.ActivationFunctionType
AX_X = mybir.AxisListType.X

P = 128
BATCH, SEQ, DIM = 2, 1024, 256
CTX, CDIM = 154, 192
HEADS, HD = 16, 16
TILE = 256
TILES = BATCH * SEQ // TILE
TB = SEQ // TILE
SUB = TILE // P
CC = DIM // P
REST = CTX - P
CPAD = P + 32
RUNS = ((0, 3), (3, 2), (5, 1))
STACK = HD * 6
DEPTH = STACK + 3
HH = HEADS // 2
UNITS = HEADS // 4
CHUNKS = 5
RESTS = 2
QBUFS = 3
MAX_BANKS, EXP_BANKS = 2, 2
GROUPS = ((0, 3), (3, 3), (6, 2), (8, 3), (11, 3), (14, 2))
NG = len(GROUPS)
MAXES = SUB * NG
KD = (P, CDIM - P)
TWO_ONES = 1.0019378662109375
EPS = 1e-5
QSCALE = HD ** -0.5


PLACES = {
    ("ln_stats", 0): -2.0143, ("ln_scale", 0): -1.9361, ("xt",): -1.7796, ("q",): -1.724, ("qsplit",): -1.636,
    ("qload",): -1.4303, ("max", 0): -0.9801, ("max", 1): -0.9048, ("max", 2): -0.8747, ("max", 3): -0.755,
    ("max", 4): -0.742, ("max", 5): -0.6691, ("max", 6): -0.6456, ("max", 7): -0.5483, ("maxsplit", 0): -0.4776,
    ("max", 8): -0.4774, ("max", 9): -0.3521, ("maxrows", 0): -0.1932, ("max", 10): -0.1876, ("max", 11): -0.0134,
    ("score", 0, 0): 0.0279, ("maxsplit", 1): 0.1262, ("score", 1, 0): 0.197, ("score", 2, 0): 0.2025,
    ("score", 3, 0): 0.2397, ("maxrows", 1): 0.2665, ("values", 0, 0): 0.2735, ("score", 4, 0): 0.3603,
    ("score", 0, 1): 0.4659, ("score", 1, 1): 0.5069, ("score", 2, 1): 0.6299, ("values", 1, 0): 0.7757,
    ("numerators", 0): 0.8015, ("score", 3, 1): 0.9025, ("values", 0, 1): 0.9149, ("score", 4, 1): 0.982,
    ("nload", 0): 0.9884, ("values", 1, 1): 1.0911, ("numerators", 1): 1.1559, ("sums",): 1.2023, ("nload", 1): 1.2169,
    ("recip",): 1.2764, ("rload",): 1.3119, ("scale",): 1.6005, ("resid",): 1.8289, ("proj",): 1.8463,
    ("ln_stats", 1): 1.8543, ("ln_scale", 1): 1.8895, ("x2t",): 2.0355, ("diff",): 2.1567, ("mixed",): 2.2453,
    ("key",): 2.4346, ("gate",): 2.5798, ("val",): 2.8869, ("out",): 3.2795,
}
SETUPS = ("identity", "k_pad", "v_ones", "k0_rows", "q_rows0", "identity_b", "q_rows1", "k_rows", "q_rows2", "first_token")
OWN_PLACES = {
    ("setup", 0): -3.4839, ("ln_stats", 0, 0): -3.3296, ("ln_scale", 0, 0): -3.1284, ("warm", 10, 0): -3.0339,
    ("setup", 1): -3.0135, ("k", 0, 0): -2.9825, ("xt", 0): -2.9824, ("k", 1, 0): -2.9823, ("ln_stats", 0, 1): -2.9791,
    ("q", 0): -2.9677, ("ln_scale", 0, 1): -2.9489, ("ksplit", 0): -2.9471, ("qsplit", 0): -2.9309, ("setup", 2): -2.9229,
    ("xt", 1): -2.9143, ("setup", 3): -2.9108, ("kload", 0): -2.9104, ("q", 1): -2.8956, ("qload", 0): -2.8763,
    ("setup", 4): -2.87, ("setup", 5): -2.8515, ("setup", 6): -2.82, ("setup", 7): -2.7868, ("setup", 8): -2.7859,
    ("qsplit", 1): -2.7433, ("setup", 9): -2.6784, ("v", 0): -2.5264, ("xload", 3): -2.486, ("kload2", 0): -2.2957,
    ("warm", 2, 0): -2.1366, ("warm", 3, 0): -2.1118, ("xload", 4): -0.3096, ("wload", 0): 0.1669, ("xload", 5): 0.1796,
    ("score", 2, 0, 0): 0.2402, ("q", 2): 0.2528, ("score", 3, 0, 0): 0.2663, ("xload", 6): 0.267,
    ("maxrows", 1, 0): 0.2852, ("values", 0, 0, 0): 0.3915, ("xload", 7): 0.4018, ("maxrows", 0, 1): 0.7722,
    ("wscale", 0): 0.9116, ("score", 4, 1, 0): 0.9391, ("values", 1, 1, 0): 0.9451, ("kstore2", 0): 1.0,
    ("nload", 0, 0): 1.0058, ("score", 0, 0, 1): 1.0079, ("kload3", 0): 1.42, ("kload4", 0): 1.43,
    ("ln_scale", 1, 0): 1.9659, ("values", 1, 1, 1): 2.0072, ("score", 0, 0, 2): 2.0508, ("gate", 0): 2.4809,
    ("max", 3, 7): 6.1623, ("values", 1, 0, 7): 7.4151, ("score", 2, 1, 7): 7.586, ("score", 3, 1, 7): 7.5923,
    ("numerators", 0, 7): 7.7642, ("values", 0, 1, 7): 7.7989, ("score", 4, 1, 7): 7.8673, ("direct", 0, 7): 7.9944,
    ("x2t", 6): 8.1605, ("diff", 6): 8.1606, ("warm", 4, 7): 8.2599, ("direct", 1, 7): 8.3102, ("warm", 5, 7): 8.8586,
    ("val", 6): 8.9811, ("warm", 3, 7): 9.2124, ("warm", 1, 7): 9.235,
}


def schedule():
    placed = {step + (T,): T + offset for step, offset in PLACES.items() for T in range(TILES)}
    placed.update(OWN_PLACES)
    for step in ("sums", "recip", "rload", "scale"):
        placed.pop((step, TILES - 1))
    return sorted(placed, key=lambda step: placed[step])


def shared_bank_uses(steps):
    number = {}
    for s in steps:
        uses = [("vmain",), ("vrest",)] if s[0] == "v" else [s]
        if s[0] in ("k", "v", "xt", "q", "maxrows", "proj", "x2t", "key", "gate", "val"):
            for use in uses:
                number[use] = len(number)
    return number


def build(nc, x, ctx_t, q_w, vecs, kv_w, kv_b, proj_w, proj_b, wr_t, wk_t, wv_t, out):
    STEPS = schedule()
    USE = shared_bank_uses(STEPS)

    with ExitStack() as stack:
        def sb(name, shape, dt=F32):
            return stack.enter_context(nc.sbuf_tensor(name, shape, dt))

        def ps(name, shape, dt=F32):
            return stack.enter_context(nc.psum_tensor(name, shape, dt))

        def sem(name):
            return stack.enter_context(nc.semaphore(name))

        x_nat = sb("x_nat", [P, TILES, SUB, DIM])
        xn = sb("xn", [P, SUB, DIM])
        xnT = sb("xnT", [P, CC, TILE])
        wq = sb("wq", [P, CC, DIM])
        wkv = sb("wkv", [P, 2, 2 * DIM])
        wp = sb("wp", [P, CC, DIM])
        wr = sb("wr", [P, CC, DIM])
        wk = sb("wk", [P, CC, DIM])
        wv = sb("wv", [P, CC, DIM])
        ctxT = sb("ctxT", [P, 2, BATCH * CTX])
        cols = sb("cols", [P, 5, CC])
        vbias = sb("vbias", [P, DIM])
        pbias = sb("pbias", [P, DIM])
        ident = sb("ident", [P, P])
        identb = sb("identb", [P, P], BF16)
        stats = sb("stats", [P, SUB, 6])
        mv = sb("mv", [P, 2, SUB, 2])
        vare = sb("vare", [P, 2, SUB])
        rstd = sb("rstd", [P, 2, SUB])
        warm = sb("warm", [P, 1])
        halves = sb("halves", [P, SUB])
        kf = sb("kf", [P, CC, BATCH * CTX])
        kr = sb("kr", [P, CC, BATCH * CTX])
        kparts = sb("kparts", [P, BATCH, 3, CC, CPAD], BF16)
        qf = sb("qf", [P, CC, TILE])
        qr = sb("qr", [P, CC, TILE])
        qparts = sb("qparts", [P, 2, 3, CC, TILE], BF16)
        kstack = sb("kstack", [P, BATCH, HEADS, CPAD], BF16)
        kstack0 = sb("kstack0", [P, BATCH, HEADS, CPAD], BF16)
        qstack = sb("qstack", [P, QBUFS, HEADS, TILE], BF16)
        vmain = sb("vmain", [P, BATCH, HEADS, 32])
        vrest = sb("vrest", [P, BATCH, UNITS, P])
        nmax = sb("nmax", [P, SUB, HEADS])
        nmaxr = sb("nmaxr", [P, SUB, HEADS])
        mparts = sb("mparts", [P, 2, SUB, 3, HH], BF16)
        mT = sb("mT", [3 * HH, 2, TILE], BF16)
        probs = sb("probs", [P, 2, CHUNKS, 2, TILE])
        pvout = sb("pvout", [P, 2, 2, TILE])
        sums = sb("sums", [P, HEADS * TILE // P])
        rsums = sb("rsums", [P, HEADS * TILE // P])
        attn = sb("attn", [P, 2, CC, TILE])
        rbc = sb("rbc", [P, CC, TILE])
        lsum = sb("lsum", [P, CC, TILE])
        lrec = sb("lrec", [P, CC, TILE])
        xn2 = sb("xn2", [P, SUB, DIM])
        zeros = sb("zeros", [P, 512], BF16)
        x2 = sb("x2", [P, 2, SUB, DIM])
        xn2T = sb("xn2T", [P, 2, CC, TILE + 1])
        diff = sb("diff", [P, CC, TILE])
        xr = sb("xr", [P, CC, TILE])
        xk = sb("xk", [P, CC, TILE])
        kact = sb("kact", [P, CC, TILE])
        gate = sb("gate", [P, SUB, DIM])
        y = sb("y", [P, SUB, DIM])
        relu = diff

        kd = nc.dram_tensor("k_parts_d", [BATCH, 3, HD, HEADS, CPAD], BF16, kind="Internal").ap()
        qd = nc.dram_tensor("q_parts_d", [2, 3, HD, HEADS, TILE], BF16, kind="Internal").ap()
        pvd = nc.dram_tensor("pv_d", [2, HEADS, 32, TILE], F32, kind="Internal").ap()
        rsd = nc.dram_tensor("rsums_d", [2, HEADS, TILE], F32, kind="Internal").ap()

        shared = [ps(f"shared{n}", [P, 512]) for n in range(2)]
        smax = [ps(f"smax{n}", [P, 512]) for n in range(MAX_BANKS)]
        sexp = [ps(f"sexp{n}", [P, 512]) for n in range(EXP_BANKS)]
        pv = [ps(f"pv{n}", [P, 512]) for n in range(2)]

        x_in = [sem(f"x_in{t}") for t in range(TILES)]
        cols_in = sem("cols_in")
        wq_in = sem("wq_in")
        vbias_in = sem("vbias_in")
        wkv_in = sem("wkv_in")
        wlate_in = sem("wlate_in")
        setup_ok = sem("setup_ok")
        filled = [sem(f"filled{n}") for n in range(2)]
        emptied = [sem(f"emptied{n}") for n in range(2)]
        v_step = sem("v_step")
        g_step = sem("g_step")
        a_step = sem("a_step")
        var_ok = sem("var_ok")
        rstd_ok = sem("rstd_ok")
        xn_ok = sem("xn_ok")
        kparts_ok = sem("kparts_ok")
        kd_ok = [sem(f"kd_ok{b}") for b in range(BATCH)]
        kstack0_ok = [sem(f"kstack0_ok{b}") for b in range(BATCH)]
        kstack_ok = [sem(f"kstack_ok{b}") for b in range(BATCH)]
        v_ok = sem("v_ok")
        qparts_ok = sem("qparts_ok")
        qd_ok = sem("qd_ok")
        qstack_ok = [sem(f"qstack_ok{n}") for n in range(QBUFS)]
        smax_full = sem("smax_full")
        smax_read = sem("smax_read")
        mparts_ok = sem("mparts_ok")
        mT_ok = sem("mT_ok")
        mrows_ok = [sem(f"mrows_ok{n}") for n in range(2)]
        sexp_full = sem("sexp_full")
        exp_ok = sem("exp_ok")
        pv_full = sem("pv_full")
        pvout_ok = sem("pvout_ok")
        pvd_ok = [sem(f"pvd_ok{n}") for n in range(2)]
        lsum_in = [sem(f"lsum_in{n}") for n in range(2)]
        sums_ok = [sem(f"sums_ok{n}") for n in range(2)]
        zeros_ok = sem("zeros_ok")
        rsums_ok = sem("rsums_ok")
        rsd_ok = [sem(f"rsd_ok{n}") for n in range(2)]
        rbc_ok = [sem(f"rbc_ok{n}") for n in range(2)]
        attn_in = [[sem(f"attn_in{n}_{half}") for half in range(2)] for n in range(2)]
        attn_ok = sem("attn_ok")
        x2_ok = sem("x2_ok")
        resid_ok = sem("resid_ok")
        xn2_ok = sem("xn2_ok")
        xn2T_ok = sem("xn2T_ok")
        diff_ok = sem("diff_ok")
        mixed_ok = sem("mixed_ok")
        kact_ok = sem("kact_ok")
        wv_ok = sem("wv_ok")
        gated_ok = sem("gated_ok")
        y_ok = sem("y_ok")
        y_out = sem("y_out")

        x_d = x.rearrange("b (t s p) c -> (b t) p s c", s=SUB, p=P)
        out_d = out.rearrange("b (t s p) c -> (b t) p s c", s=SUB, p=P)

        def maximum(n):
            half = n // (MAXES // 2)
            return half, n % (MAXES // 2) // (NG // 2), half * (NG // 2) + n % (NG // 2)

        def bank(*use):
            return shared[USE[use] % 2]

        def may_fill(eng, *use):
            n = USE[use]
            if n >= 2:
                eng.wait_ge(emptied[n % 2], n // 2)

        def fill(ins, *use):
            ins.then_inc(filled[USE[use] % 2], 1)

        def await_bank(eng, *use):
            n = USE[use]
            eng.wait_ge(filled[n % 2], n // 2 + 1)

        def empty(ins, *use):
            ins.then_inc(emptied[USE[use] % 2], 1)

        def last_token(T):
            return xn2T[:, T % 2, :, 0:1], xn2T[:, (T - 1) % 2, :, TILE:TILE + 1]

        def difference(T, c):
            return diff[:, c, :], xn2T[:, T % 2, c, 1:TILE + 1], xn2T[:, T % 2, c, 0:TILE]

        def await_setup(eng, name):
            eng.wait_ge(setup_ok, SETUPS.index(name) + 1)

        block = stack.enter_context(nc.Block())

        @block.sync
        def _(sp):
            sp.dma_start(x_nat[:, 0], x_d[0]).then_inc(x_in[0], 16)
            for k in range(2):
                sp.dma_start(ctxT[0:KD[k], k, :], ctx_t[k * P:k * P + KD[k], :]).then_inc(wkv_in, 16)
                sp.dma_start(wkv[0:KD[k], k, :], kv_w[k * P:k * P + KD[k], :]).then_inc(wkv_in, 16)
            sp.dma_start(cols[:, 0:4, :], vecs).then_inc(cols_in, 16)
            sp.dma_start(wq[:, :, :], q_w.rearrange("(c p) n -> p c n", p=P)).then_inc(wq_in, 16)
            sp.dma_start(x_nat[:, 1], x_d[1]).then_inc(x_in[1], 16)
            sp.dma_start(vbias[:, :], kv_b[DIM:2 * DIM].partition_broadcast(P)).then_inc(vbias_in, 16)
            sp.dma_start(x_nat[:, 2], x_d[2]).then_inc(x_in[2], 16)

            def store_k(b):
                sp.dma_start(kd[b].rearrange("a (m d) h n -> (d h) (a m) n", m=CC),
                             kparts[:, b].rearrange("p a m n -> p (a m) n")).then_inc(kd_ok[b], 16)

            def load_k(target, b, loaded):
                for n, parts in RUNS:
                    sp.dma_start(target[HD * n:HD * (n + parts), b, :, :].rearrange("p h n -> p (h n)"),
                                 kd[b, 0:parts].rearrange("a d h n -> (a d) (h n)")).then_inc(loaded[b], 16)

            for s in STEPS:
                stage, T = s[0], s[-1]
                if stage == "ksplit":
                    sp.wait_ge(kparts_ok, 1)
                    store_k(0)
                if stage == "kload":
                    sp.wait_ge(kd_ok[0], 16)
                    load_k(kstack0, 0, kstack0_ok)
                if stage == "qsplit":
                    sp.wait_ge(qparts_ok, T + 1)
                    sp.dma_start(qd[T % 2].rearrange("a (m d) h n -> (d h) (a m) n", m=CC),
                                 qparts[:, T % 2, :, :, :].rearrange("p a m n -> p (a m) n")).then_inc(qd_ok, 16)
                if stage == "qload":
                    sp.wait_ge(qd_ok, 16 * (T + 1))
                    if T >= QBUFS:
                        sp.wait_ge(sexp_full, 2 * CHUNKS * (T - QBUFS + 1))
                    for part, (n, copies) in enumerate(RUNS):
                        sp.dma_start(qstack[HD * n:HD * (n + copies), T % QBUFS, :, :].rearrange("p h n -> p (h n)"),
                                     qd[T % 2, part:part + 1].rearrange("a d h n -> a d (h n)").to_broadcast([copies, HD, HEADS * TILE])
                                     ).then_inc(qstack_ok[T % QBUFS], 16)
                if stage == "kload2":
                    load_k(kstack, 0, kstack_ok)
                if stage == "kstore2":
                    store_k(1)
                if stage == "kload3":
                    sp.wait_ge(kd_ok[1], 16)
                    load_k(kstack0, 1, kstack0_ok)
                if stage == "kload4":
                    load_k(kstack, 1, kstack_ok)
                if stage == "xload":
                    sp.dma_start(x_nat[:, T], x_d[T]).then_inc(x_in[T], 16)
                if stage == "wload":
                    for w_sb, w_d in ((wp, proj_w), (wr, wr_t), (wk, wk_t), (wv, wv_t)):
                        sp.dma_start(w_sb[:, :, :], w_d.rearrange("(c p) n -> p c n", p=P)).then_inc(wlate_in, 16)
                    sp.dma_start(pbias[:, :], proj_b.partition_broadcast(P)).then_inc(wlate_in, 16)
                if stage == "maxrows":
                    half = s[1]
                    sp.wait_ge(mT_ok, 2 * T + half + 1)
                    if T < QBUFS:
                        await_setup(sp, f"q_rows{T}")
                    sp.dma_start(qstack[STACK:DEPTH, T % QBUFS, HH * half:HH * (half + 1), :], mT[:, half, :]).then_inc(mrows_ok[half], 16)
                if stage == "numerators":
                    half = s[1]
                    sp.wait_ge(pvout_ok, 2 * T + half + 1)
                    sp.dma_start(pvd[T % 2, HH * half:HH * (half + 1)].rearrange("(u h) r n -> (h r) u n", u=2),
                                 pvout[:, half, :, :]).then_inc(pvd_ok[half], 16)
                if stage == "nload":
                    half = s[1]
                    sp.wait_ge(pvd_ok[half], 16 * (T + 1))
                    if T == TILES - 1:
                        sp.dma_start(lsum[:, half, :], pvd[T % 2, HH * half:HH * (half + 1), HD:2 * HD, :]).then_inc(lsum_in[half], 16)
                    if T >= 2:
                        await_bank(sp, "proj", T - 2)
                    sp.dma_start(attn[:, T % 2, half, :], pvd[T % 2, HH * half:HH * (half + 1), 0:HD, :]).then_inc(attn_in[T % 2][half], 16)
                if stage == "sums":
                    for n in range(2):
                        sp.wait_ge(pvd_ok[n], 16 * (T + 1))
                    if T >= 1:
                        sp.wait_ge(rsums_ok, T)
                    sp.dma_start(sums[:, :], pvd[T % 2, :, HD, :].rearrange("h (c n) -> h c n", n=HEADS * TILE // P)).then_inc(sums_ok[T % 2], 16)
                if stage == "recip":
                    sp.wait_ge(rsums_ok, T + 1)
                    sp.dma_start(rsd[T % 2].rearrange("h (c n) -> h c n", n=HEADS * TILE // P), rsums[:, :]).then_inc(rsd_ok[T % 2], 16)
                if stage == "rload":
                    sp.wait_ge(rsd_ok[T % 2], 16 * (T // 2 + 1))
                    if T >= 1:
                        sp.wait_ge(attn_ok, T)
                    for c in range(CC):
                        sp.dma_start(rbc[:, c, :],
                                     rsd[T % 2, 8 * c:8 * c + 8, :].rearrange("h (o n) -> h o n", o=1).to_broadcast([8, HD, TILE])
                                     ).then_inc(rbc_ok[T % 2], 16)
                if stage == "out":
                    sp.wait_ge(y_ok, T + 1)
                    sp.dma_start(out_d[T], y[:, :, :]).then_inc(y_out, 16)
            sp.wait_ge(y_out, 16 * TILES)

        @block.gpsimd
        def _(pool):
            steps = [0]

            def step(ins):
                ins.then_inc(g_step, 1)
                steps[0] += 1
                pool.wait_ge(g_step, steps[0])

            norms = [0]

            def identity(t):
                step(nc.gpsimd.memset(t[:, :], 0.0))
                step(nc.gpsimd.affine_select(out=t[:, :], in_=t[:, :], compare_op=ALU.not_equal, fill=1.0,
                                             base=0, pattern=[[-1, P]], channel_multiplier=1))

            def setup(name):
                if norms[0]:
                    pool.wait_ge(rstd_ok, norms[0])
                if name == "identity":
                    identity(ident)
                if name == "identity_b":
                    identity(identb)
                if name == "k_pad":
                    step(nc.gpsimd.memset(kparts[:, :, :, :, CTX:CPAD], 0.0))
                if name in ("k0_rows", "k_rows"):
                    t = kstack if name == "k_rows" else kstack0
                    step(nc.gpsimd.memset(t[STACK:P].rearrange("p b h n -> p (b h n)").bitcast(F32), 0.0))
                if name == "k_rows":
                    ones = kstack[STACK:DEPTH, :, :, :].rearrange("p b h n -> p (b h) n").bitcast(F32)
                    step(nc.gpsimd.memset(ones[:, :, 0:CTX // 2], TWO_ONES))
                if name[:-1] == "q_rows":
                    step(nc.gpsimd.memset(qstack[STACK:P, int(name[-1])].rearrange("p h n -> p (h n)").bitcast(F32), 0.0))
                if name == "v_ones":
                    nc.gpsimd.memset(vmain[:, :, :, HD:32], 1.0)
                    step(nc.gpsimd.memset(vrest[:, :, :, :], 0.0))
                    for j in range(4):
                        step(nc.gpsimd.memset(vrest[32 * j:32 * j + REST, :, :, 32 * j + HD:32 * j + 32], 1.0))
                if name == "first_token":
                    step(nc.gpsimd.memset(xn2T[:, 0, :, 0:1], 0.0))
                pool.sem_inc(setup_ok, 1)

            step(nc.gpsimd.memset(halves[:, :], -0.5))
            for s in STEPS:
                stage, T = s[0], s[-1]
                if stage == "ln_stats":
                    which = s[1]
                    norms[0] += 1
                    pool.wait_ge(var_ok, norms[0])
                    nc.gpsimd.tensor_tensor(rstd[:, which, :], vare[:, which, :], halves[:, :], ALU.pow).then_inc(rstd_ok, 1)
                if stage == "setup":
                    setup(SETUPS[s[1]])
                if stage == "resid":
                    pool.wait_ge(xn_ok, T + 1)
                    if T == 0:
                        pool.wait_ge(wlate_in, 16 * 5)
                    for t in range(SUB):
                        last = nc.gpsimd.tensor_tensor(x_nat[:, T, t, :], x_nat[:, T, t, :], pbias[:, :], ALU.add)
                    last.then_inc(resid_ok, 1)
                if stage == "out" and T < TILES - 1:
                    pool.wait_ge(gated_ok, T + 1)
                    if T >= 1:
                        pool.wait_ge(y_out, 16 * T)
                    for t in range(SUB):
                        last = nc.gpsimd.tensor_tensor(y[:, t, :], gate[:, t, :], x2[:, T % 2, t, :], ALU.add)
                    last.then_inc(y_ok, 1)
                if stage == "diff" and T < TILES - 1:
                    pool.wait_ge(xn2T_ok, T + 1)
                    if T >= 1:
                        pool.wait_ge(kact_ok, T)
                    if T % TB:
                        step(nc.gpsimd.tensor_copy(*last_token(T)))
                    elif T:
                        step(nc.gpsimd.memset(xn2T[:, T % 2, :, 0:1], 0.0))
                    for c in range(CC):
                        nc.gpsimd.tensor_tensor(*difference(T, c), ALU.subtract).then_inc(diff_ok, 1)

        @block.scalar
        def _(act):
            act.wait_ge(g_step, 1)
            nc.scalar.activation(warm[:, :], halves[:, 0:1], ACT.Exp)
            for s in STEPS:
                stage, T = s[0], s[-1]
                if stage == "k":
                    m = s[1]
                    act.wait_ge(cols_in, 16)
                    await_bank(act, *s)
                    empty(nc.scalar.activation(kf[:, m, :], bank(*s)[:, 0:BATCH * CTX], ACT.Identity, bias=cols[:, 1, m:m + 1]), *s)
                if stage == "xt":
                    await_bank(act, *s)
                    if T >= 1:
                        await_bank(act, "q", T - 1)
                    empty(nc.scalar.copy(xnT[:, :, :].rearrange("p c n -> p (c n)"), bank(*s)[:, :]), *s)
                if stage == "q":
                    if T == 0:
                        act.wait_ge(a_step, 1)
                    await_bank(act, *s)
                    if T >= 1:
                        act.wait_ge(qparts_ok, T)
                    if T >= 2:
                        act.wait_ge(qd_ok, 16 * (T - 1))
                    for target in (qf, qparts[:, T % 2, 0]):
                        for m in range(CC):
                            last = nc.scalar.activation(target[:, m, :], bank(*s)[:, m * TILE:(m + 1) * TILE], ACT.Identity,
                                                        bias=cols[:, 4, m:m + 1], scale=QSCALE)
                    empty(last, *s)
                if stage == "maxrows":
                    half = s[1]
                    await_bank(act, *s)
                    if T >= 1:
                        act.wait_ge(mrows_ok[half], 16 * T)
                    nc.scalar.copy(mT[:, half, :], bank(*s).bitcast(BF16)[0:3 * HH, 0:TILE]).then_inc(mT_ok, 1)
                    act.wait_ge(mT_ok, 2 * T + half + 1)
                    act.sem_inc(emptied[USE[s] % 2], 1)
                if stage == "score":
                    c, half = s[1:3]
                    H = 2 * T + half
                    n = CHUNKS * H + c
                    act.wait_ge(sexp_full, n + 1)
                    if T >= 1 and c == 0:
                        act.wait_ge(pv_full, H - 1)
                    nc.scalar.activation(probs[:, half, c, :, :].rearrange("p a n -> p (a n)"), sexp[n % EXP_BANKS][:, :],
                                         ACT.Exp).then_inc(exp_ok, 1)
                if stage == "numerators":
                    half = s[1]
                    H = 2 * T + half
                    act.wait_ge(pv_full, H + 1)
                    if T >= 1:
                        act.wait_ge(pvd_ok[half], 16 * T)
                    nc.scalar.copy(pvout[:, half, :, :].rearrange("p u n -> p (u n)"), pv[half][:, :]).then_inc(pvout_ok, 1)
                if stage == "x2t":
                    await_bank(act, *s)
                    if T >= 2:
                        act.wait_ge(mixed_ok, 2 * (T - 1))
                        act.wait_ge(diff_ok, CC * T)
                    nc.scalar.copy(xn2T[:, T % 2, :, 1:TILE + 1],
                                   bank(*s)[:, :].rearrange("p (c n) -> p c n", c=CC)).then_inc(xn2T_ok, 1)
                    act.wait_ge(xn2T_ok, T + 1)
                    act.sem_inc(emptied[USE[s] % 2], 1)
                if stage == "key":
                    await_bank(act, *s)
                    act.wait_ge(mixed_ok, 2 * (T + 1))
                    empty(nc.scalar.activation(relu[:, :, :].rearrange("p c n -> p (c n)"), bank(*s)[:, :], ACT.Relu), *s)
                    act.wait_ge(emptied[USE[s] % 2], USE[s] // 2 + 1)
                    if T >= 1:
                        act.wait_ge(y_ok, T)
                    nc.scalar.activation(kact[:, :, :], relu[:, :, :], ACT.Square).then_inc(kact_ok, 1)
                if stage == "gate":
                    await_bank(act, *s)
                    empty(nc.scalar.activation(gate[:, :, :].rearrange("p s c -> p (s c)"), bank(*s)[:, :], ACT.Tanh, scale=0.5), *s)

        @block.vector
        def _(dve):
            steps = [0]

            def step(ins):
                ins.then_inc(v_step, 1)
                steps[0] += 1
                dve.wait_ge(v_step, steps[0])

            norms = [0]
            nc.vector.memset(zeros[:, :], 0.0).then_inc(zeros_ok, 1)

            def split(whole, left, parts):
                step(nc.vector.tensor_copy(parts[0], whole))
                return split_rest(whole, left, parts)

            def split_rest(whole, left, parts):
                step(nc.vector.tensor_tensor(left, whole, parts[0], ALU.subtract))
                step(nc.vector.tensor_copy(parts[1], left))
                return nc.vector.tensor_tensor(parts[2], left, parts[1], ALU.subtract)

            def read(use):
                dve.wait_ge(emptied[USE[use] % 2], USE[use] // 2 + 1)

            for s in STEPS:
                stage, T = s[0], s[-1]
                if stage == "ln_stats":
                    which = s[1]
                    source = x_nat[:, T] if which == 0 else x2[:, T % 2]
                    if which == 0:
                        dve.wait_ge(x_in[T], 16)
                    for t in range(SUB):
                        last = nc.vector.bn_stats(out=stats[:, t, :], in_=source[:, t, :])
                    step(last)
                    for t in range(SUB):
                        last = nc.vector.bn_aggr(out=mv[:, which, t, :], in_=stats[:, t, :])
                    step(last)
                    nc.vector.tensor_scalar_add(vare[:, which, :], mv[:, which, :, 1], EPS).then_inc(var_ok, 1)
                if stage == "ln_scale":
                    which = s[1]
                    source = x_nat[:, T] if which == 0 else x2[:, T % 2]
                    target = xn if which == 0 else xn2
                    if which == 0 and T >= 1:
                        await_bank(dve, "xt", T - 1)
                    norms[0] += 1
                    dve.wait_ge(rstd_ok, norms[0])
                    for t in range(SUB):
                        last = nc.vector.tensor_scalar(target[:, t, :], source[:, t, :], mv[:, which, t, 0:1],
                                                       rstd[:, which, t:t + 1], ALU.subtract, ALU.mult)
                    last.then_inc(xn_ok if which == 0 else xn2_ok, 1)
                if stage == "k" and s[1] == 0:
                    dve.wait_ge(cols_in, 16)
                    nc.vector.tensor_scalar_mul(cols[:, 4, :], cols[:, 0, :], QSCALE).then_inc(a_step, 1)
                if stage == "ksplit":
                    for m in range(CC):
                        read(("k", m, 0))
                    await_setup(dve, "k_pad")
                    split(kf[:, :, :].rearrange("p m (b n) -> p b m n", b=BATCH),
                          kr[:, :, :].rearrange("p m (b n) -> p b m n", b=BATCH),
                          [kparts[:, :, a, :, 0:CTX] for a in range(3)]).then_inc(kparts_ok, 1)
                if stage == "v":
                    dve.wait_ge(vbias_in, 16)
                    await_bank(dve, "vmain")
                    for b in range(BATCH):
                        last = nc.vector.tensor_tensor(
                            vmain[:, b, :, 0:HD], bank("vmain")[:, b * DIM:(b + 1) * DIM].rearrange("p (h d) -> p h d", d=HD),
                            vbias[:, :].rearrange("p (h d) -> p h d", d=HD), ALU.add)
                    empty(last, "vmain")
                    await_bank(dve, "vrest")
                    await_setup(dve, "v_ones")
                    for j in range(4):
                        rows = slice(32 * j, 32 * j + REST)
                        for b in range(BATCH):
                            last = nc.vector.tensor_tensor(
                                vrest[rows, b, :, 32 * j:32 * j + HD],
                                bank("vrest")[rows, b * 64:(b + 1) * 64].rearrange("p (g d) -> p g d", d=HD),
                                vbias[rows, :].rearrange("p (g j d) -> p j g d", j=4, d=HD)[:, j], ALU.add)
                    step(last)
                    dve.sem_inc(v_ok, 1)
                    dve.sem_inc(emptied[USE[("vrest",)] % 2], 1)
                if stage == "qsplit":
                    read(("q", T))
                    split_rest(qf[:, :, :], qr[:, :, :], [qparts[:, T % 2, a, :, :] for a in range(3)]).then_inc(qparts_ok, 1)
                if stage == "max":
                    half, t, g = maximum(s[1])
                    h0, nh = GROUPS[g]
                    n = T * MAXES + s[1]
                    dve.wait_ge(smax_full, n + 1)
                    if T >= 1 and t == 0:
                        dve.wait_ge(mparts_ok, 2 * T - 1 + half)
                    nc.vector.tensor_reduce(nmax[:, t, h0:h0 + nh],
                                            smax[n % MAX_BANKS][:, 0:nh * CTX].rearrange("p (h n) -> p h n", n=CTX),
                                            AX_X, ALU.max, negate=True).then_inc(smax_read, 1)
                if stage == "maxsplit":
                    half = s[1]
                    dve.wait_ge(smax_read, T * MAXES + (half + 1) * MAXES // 2)
                    if T >= 1:
                        await_bank(dve, "maxrows", half, T - 1)
                    hs = slice(HH * half, HH * (half + 1))
                    split(nmax[:, :, hs], nmaxr[:, :, hs], [mparts[:, half, :, a, :] for a in range(3)]).then_inc(mparts_ok, 1)
                if stage == "recip":
                    dve.wait_ge(sums_ok[T % 2], 16 * (T // 2 + 1))
                    if T >= 1:
                        dve.wait_ge(rsd_ok[(T - 1) % 2], 16 * ((T - 1) // 2 + 1))
                    nc.vector.reciprocal(rsums[:, :], sums[:, :]).then_inc(rsums_ok, 1)
                if stage == "scale":
                    for half in range(2):
                        dve.wait_ge(attn_in[T % 2][half], 16 * (T // 2 + 1))
                    dve.wait_ge(rbc_ok[T % 2], 32 * (T // 2 + 1))
                    nc.vector.tensor_tensor(attn[:, T % 2, :, :], attn[:, T % 2, :, :], rbc[:, :, :], ALU.mult).then_inc(attn_ok, 1)
                if stage == "direct":
                    half = s[1]
                    dve.wait_ge(lsum_in[half], 16)
                    step(nc.vector.reciprocal(lrec[:, half, :], lsum[:, half, :]))
                    dve.wait_ge(attn_in[T % 2][half], 16 * (T // 2 + 1))
                    last = nc.vector.tensor_tensor(attn[:, T % 2, half, :], attn[:, T % 2, half, :], lrec[:, half, :], ALU.mult)
                    step(last)
                    if half:
                        dve.sem_inc(attn_ok, 1)
                if stage == "proj":
                    dve.wait_ge(resid_ok, T + 1)
                    if T >= 2:
                        dve.wait_ge(y_ok, T - 1)
                    await_bank(dve, *s)
                    nc.vector.tensor_tensor(x2[:, T % 2, :, :].rearrange("p s c -> p (s c)"), bank(*s)[:, :],
                                            x_nat[:, T, :, :].rearrange("p s c -> p (s c)"), ALU.add).then_inc(x2_ok, 1)
                    dve.wait_ge(x2_ok, T + 1)
                    dve.sem_inc(emptied[USE[s] % 2], 1)
                if stage == "diff" and T == TILES - 1:
                    dve.wait_ge(xn2T_ok, T + 1)
                    dve.wait_ge(kact_ok, T)
                    step(nc.vector.tensor_copy(*last_token(T)))
                    for c in range(CC):
                        nc.vector.tensor_tensor(*difference(T, c), ALU.subtract).then_inc(diff_ok, 1)
                if stage == "mixed":
                    dve.wait_ge(diff_ok, CC * (T + 1))
                    if T >= 1:
                        await_bank(dve, "gate", T - 1)
                    for target, n in ((xk, 3), (xr, 2)):
                        for c in range(CC):
                            last = nc.vector.scalar_tensor_tensor(
                                out=target[:, c, :], in0=diff[:, c, :], scalar=cols[:, n, c:c + 1],
                                in1=xn2T[:, T % 2, c, 0:TILE], op0=ALU.mult, op1=ALU.add)
                        last.then_inc(mixed_ok, 1)
                if stage == "val":
                    read(("gate", T))
                    await_bank(dve, *s)
                    g2 = gate[:, :, :].rearrange("p s c -> p (s c)")
                    nc.vector.scalar_tensor_tensor(out=g2, in0=g2, scalar=1.0, in1=bank(*s)[:, :],
                                                   op0=ALU.add, op1=ALU.mult).then_inc(gated_ok, 1)
                    dve.wait_ge(gated_ok, T + 1)
                    dve.sem_inc(emptied[USE[s] % 2], 1)
                if stage == "out" and T == TILES - 1:
                    dve.wait_ge(y_out, 16 * T)
                    nc.vector.tensor_tensor(y[:, :, :], gate[:, :, :], x2[:, T % 2, :, :], ALU.add).then_inc(y_ok, 1)
                if stage == "wscale":
                    dve.wait_ge(wlate_in, 16 * 5)
                    nc.vector.tensor_scalar_mul(wv[:, :, :], wv[:, :, :], 0.5).then_inc(wv_ok, 1)

        @block.tensor
        def _(pe):
            def transposes(source, *use):
                may_fill(pe, *use)
                for c in range(CC):
                    for t in range(SUB):
                        last = nc.tensor.transpose(bank(*use)[:, c * TILE + t * P:c * TILE + (t + 1) * P],
                                                   source[:, t, c * P:(c + 1) * P], ident[:, :])
                fill(last, *use)

            def natural(lhs, w, *use):
                may_fill(pe, *use)
                for t in range(SUB):
                    for k in range(CC):
                        last = nc.tensor.matmul(bank(*use)[:, t * DIM:(t + 1) * DIM], lhs[:, k, t * P:(t + 1) * P], w[:, k, :],
                                                start=(k == 0), stop=(k == CC - 1))
                fill(last, *use)

            def channels(w, rhs, *use):
                may_fill(pe, *use)
                for m in range(CC):
                    for k in range(CC):
                        last = nc.tensor.matmul(bank(*use)[:, m * TILE:(m + 1) * TILE], w[:, k, m * P:(m + 1) * P], rhs[:, k, :],
                                                start=(k == 0), stop=(k == CC - 1))
                fill(last, *use)

            for s in STEPS:
                stage, T = s[0], s[-1]
                if stage == "warm":
                    pe.wait_ge(zeros_ok, 1)
                    if T == TILES - 1:
                        pe.wait_ge(smax_read, TILES * MAXES)
                    for _ in range(s[1]):
                        nc.tensor.matmul(smax[0][:, :], zeros[:, 0:P], zeros[:, :], start=True, stop=True)
                if stage == "k":
                    m = s[1]
                    pe.wait_ge(wkv_in, 16 * 4)
                    may_fill(pe, *s)
                    for k in range(2):
                        last = nc.tensor.matmul(bank(*s)[:, 0:BATCH * CTX], wkv[0:KD[k], k, m * P:(m + 1) * P],
                                                ctxT[0:KD[k], k, :], start=(k == 0), stop=(k == 1))
                    fill(last, *s)
                if stage == "v":
                    may_fill(pe, "vmain")
                    for b in range(BATCH):
                        for k in range(2):
                            last = nc.tensor.matmul(bank("vmain")[:, b * DIM:(b + 1) * DIM], ctxT[0:KD[k], k, b * CTX:b * CTX + P],
                                                    wkv[0:KD[k], k, DIM:2 * DIM], start=(k == 0), stop=(k == 1))
                    fill(last, "vmain")
                    may_fill(pe, "vrest")
                    for j in range(4):
                        for b in range(BATCH):
                            for k in range(2):
                                w = wkv[0:KD[k], k, DIM:2 * DIM].rearrange("p (g j d) -> p j g d", j=4, d=HD)[:, j]
                                last = nc.tensor.matmul(bank("vrest")[32 * j:32 * j + REST, b * 64:(b + 1) * 64],
                                                        ctxT[0:KD[k], k, b * CTX + P:(b + 1) * CTX], w,
                                                        start=(k == 0), stop=(k == 1))
                    fill(last, "vrest")
                if stage == "xt":
                    if T == 0:
                        await_setup(pe, "identity")
                    pe.wait_ge(xn_ok, T + 1)
                    transposes(xn, *s)
                if stage == "q":
                    use = USE[("xt", T)]
                    pe.wait_ge(emptied[use % 2], use // 2 + 1)
                    if T == 0:
                        pe.wait_ge(wq_in, 16)
                    channels(wq, xnT, *s)
                if stage == "max":
                    half, t, g = maximum(s[1])
                    h0, nh = GROUPS[g]
                    n = T * MAXES + s[1]
                    if n % (TB * MAXES) == 0:
                        pe.wait_ge(kstack0_ok[T // TB], 16 * len(RUNS))
                    if n == 0:
                        await_setup(pe, "k0_rows")
                    if T < QBUFS and s[1] == 0:
                        await_setup(pe, f"q_rows{T}")
                    if s[1] == 0:
                        pe.wait_ge(qstack_ok[T % QBUFS], 16 * len(RUNS) * (T // QBUFS + 1))
                    if n >= MAX_BANKS:
                        pe.wait_ge(smax_read, n - MAX_BANKS + 1)
                    for k in range(nh):
                        last = nc.tensor.matmul(smax[n % MAX_BANKS][:, k * CTX:(k + 1) * CTX],
                                                qstack[:, T % QBUFS, h0 + k, t * P:(t + 1) * P],
                                                kstack0[:, T // TB, h0 + k, 0:CTX], start=True, stop=True)
                    last.then_inc(smax_full, 1)
                if stage == "maxrows":
                    half = s[1]
                    pe.wait_ge(mparts_ok, 2 * T + half + 1)
                    if T == 0:
                        await_setup(pe, "identity_b")
                    may_fill(pe, *s)
                    for t in range(SUB):
                        last = nc.tensor.transpose(bank(*s).bitcast(BF16)[0:24, t * P:(t + 1) * P],
                                                   mparts[:, half, t, :, :].rearrange("p a h -> p (a h)"), identb[:, :])
                    fill(last, *s)
                if stage == "score":
                    c, half = s[1:3]
                    if T % TB == 0 and half == 0 and c == 0:
                        pe.wait_ge(kstack_ok[T // TB], 16 * len(RUNS))
                    if T == 0 and half == 0 and c == 0:
                        await_setup(pe, "k_rows")
                    if c == 0:
                        pe.wait_ge(mrows_ok[half], 16 * (T + 1))
                    n = CHUNKS * (2 * T + half) + c
                    if n >= EXP_BANKS:
                        pe.wait_ge(exp_ok, n - EXP_BANKS + 1)
                    for a in range(2):
                        cols_a = slice(a * TILE, (a + 1) * TILE)
                        if c != RESTS:
                            h = HH * half + 2 * (c - (c > RESTS)) + a
                            last = nc.tensor.matmul(sexp[n % EXP_BANKS][:, cols_a], kstack[:, T // TB, h, 0:P], qstack[:, T % QBUFS, h, :],
                                                    start=True, stop=True)
                        else:
                            for j in range(4):
                                h = HH * half + 4 * a + j
                                last = nc.tensor.matmul(sexp[n % EXP_BANKS][32 * j:32 * j + 32, cols_a], kstack[:, T // TB, h, P:CPAD],
                                                        qstack[:, T % QBUFS, h, :], start=True, stop=True)
                    last.then_inc(sexp_full, 1)
                if stage == "values":
                    a, half = s[1:3]
                    H = 2 * T + half
                    if H == 0 and a == 0:
                        pe.wait_ge(v_ok, 1)
                    if T >= 1 and a == 0:
                        pe.wait_ge(pvout_ok, H - 1)
                    pe.wait_ge(exp_ok, CHUNKS * H + (CHUNKS if a else RESTS + 1))
                    unit = slice(a * TILE, (a + 1) * TILE)
                    for j in range(4):
                        nc.tensor.matmul(pv[half][32 * j:32 * j + 32, unit], vmain[:, T // TB, HH * half + 4 * a + j, :],
                                         probs[:, half, 3 * a + j // 2, j % 2, :], start=True, stop=False, skip_group_check=True)
                    last = nc.tensor.matmul(pv[half][:, unit], vrest[:, T // TB, 2 * half + a, :], probs[:, half, RESTS, a, :],
                                            start=False, stop=True, skip_group_check=True)
                    if a:
                        last.then_inc(pv_full, 1)
                if stage == "proj":
                    if T == 0:
                        pe.wait_ge(wlate_in, 16 * 5)
                    pe.wait_ge(attn_ok, T + 1)
                    natural(attn[:, T % 2], wp, *s)
                if stage == "x2t":
                    pe.wait_ge(xn2_ok, T + 1)
                    transposes(xn2, *s)
                if stage == "key":
                    pe.wait_ge(mixed_ok, 2 * T + 1)
                    channels(wk, xk, *s)
                if stage == "gate":
                    pe.wait_ge(mixed_ok, 2 * (T + 1))
                    natural(xr, wr, *s)
                if stage == "val":
                    if T == 0:
                        pe.wait_ge(wv_ok, 1)
                    pe.wait_ge(kact_ok, T + 1)
                    natural(kact, wv, *s)


def kernel(x, ctx_768, L0_xattn_q_w, L0_xattn_q_b, L0_xattn_kv_w, L0_xattn_kv_b, L0_xattn_proj_w, L0_xattn_proj_b,
           L0_ffn_W_r, L0_ffn_W_k, L0_ffn_W_v, L0_ffn_mu_r, L0_ffn_mu_k):
    import numpy as _np
    import concourse.bacc as _bacc
    from concourse import mybir as _mybir
    from concourse.bass_utils import run_bass_kernel_spmd as _run

    ctx = _np.asarray(ctx_768)
    kv_w = _np.asarray(L0_xattn_kv_w)

    def by_d(a):
        return _np.swapaxes(a.reshape(a.shape[:-1] + (HEADS, HD)), -1, -2).reshape(a.shape)

    laid = {
        "x": _np.asarray(x),
        "ctx_t": ctx.reshape(-1, ctx.shape[-1]).T,
        "q_w": by_d(_np.asarray(L0_xattn_q_w)),
        "vecs": _np.stack([by_d(_np.asarray(L0_xattn_q_b)), by_d(_np.asarray(L0_xattn_kv_b)[:DIM]), _np.asarray(L0_ffn_mu_r),
                           _np.asarray(L0_ffn_mu_k)]).reshape(4, CC, P).transpose(2, 0, 1),
        "kv_w": _np.concatenate([by_d(kv_w[:, :DIM]), kv_w[:, DIM:]], axis=1), "kv_b": _np.asarray(L0_xattn_kv_b),
        "proj_w": _np.asarray(L0_xattn_proj_w), "proj_b": _np.asarray(L0_xattn_proj_b),
        "wr_t": _np.asarray(L0_ffn_W_r).T, "wk_t": _np.asarray(L0_ffn_W_k).T, "wv_t": _np.asarray(L0_ffn_W_v).T,
    }
    nc = _bacc.Bacc("TRN2", target_bir_lowering=False, num_devices=1)
    arrays, args = {}, []
    for name, a in laid.items():
        a = _np.ascontiguousarray(a)
        arrays[f"in_{name}"] = a
        args.append(nc.dram_tensor(f"in_{name}", a.shape, _mybir.dt.from_np(a.dtype), kind="ExternalInput").ap())
    args.append(nc.dram_tensor("out_y", (BATCH, SEQ, DIM), _mybir.dt.float32, kind="ExternalOutput").ap())
    build(nc, *args)
    r = _run(nc, [arrays], core_ids=[0])
    return r.results[0]["out_y"]
```
